# Optimizing a Trainium2 kernel written in Bass

```python
import numpy as np
import jax
import jax.numpy as jnp

def _softmax(x, axis=-1):
    return jax.nn.softmax(x, axis=axis)

def _gelu(x):
    return jax.nn.gelu(x, approximate=True)

def _silu(x):
    return jax.nn.silu(x)

def _sigmoid(x):
    return jax.nn.sigmoid(x)

def _layernorm(x, axis=-1, eps=1e-05):
    m = jnp.mean(x, axis=axis, keepdims=True)
    v = jnp.var(x, axis=axis, keepdims=True)
    return (x - m) / jnp.sqrt(v + eps)

def _scatter_add(tgt, idx, src, axis=0):
    return tgt.at[idx].add(src)

def _segment_sum(src, seg, n):
    return jax.ops.segment_sum(src, seg, n)
kernel_name = 'mk_vit_tower_d1_tok_img256_r4_03af98'

def setup_inputs(seed: int=0):
    np.random.seed(seed)
    _w = jnp.asarray

    def _rec_inputs():
        import jax
        import jax.numpy as jnp
        _rk = jax.random.key(seed)
        x = 7.22013e-05 + 1.00017 * jax.random.normal(jax.random.fold_in(_rk, 1), (4, 1, 1024, 64), jnp.float32)
        return x
    x = _rec_inputs()

    def _L0_tok_setup():
        import jax, jax.numpy as jnp
        import numpy as np
        T, D_IN, D_INT, D_OUT, B = (1024, 64, 64, 64, 8)
        key = jax.random.key(seed)
        ks = jax.random.split(key, 12)
        s_in = 1.0 / np.sqrt(D_IN)
        s_int = 1.0 / np.sqrt(D_INT)
        return {'x_batched': jax.random.normal(ks[0], (B, 1, T, D_IN), dtype=jnp.float32), 'd_gamma_batched': jax.random.uniform(ks[1], (T, T), dtype=jnp.float32), 'Wq': jax.random.uniform(ks[2], (D_IN, D_INT), jnp.float32, -s_in, s_in), 'bq': jax.random.uniform(ks[3], (D_INT,), jnp.float32, -s_in, s_in), 'Wk': jax.random.uniform(ks[4], (D_IN, D_INT), jnp.float32, -s_in, s_in), 'bk': jax.random.uniform(ks[5], (D_INT,), jnp.float32, -s_in, s_in), 'Wv': jax.random.uniform(ks[6], (D_IN, D_INT), jnp.float32, -s_in, s_in), 'bv': jax.random.uniform(ks[7], (D_INT,), jnp.float32, -s_in, s_in), 'Wo': jax.random.uniform(ks[8], (D_INT, D_OUT), jnp.float32, -s_int, s_int), 'bo': jax.random.uniform(ks[9], (D_OUT,), jnp.float32, -s_int, s_int), 'prelu_a': jnp.float32(0.25)}
    _L0_tok_all = _L0_tok_setup()
    _L0_tok_in = {k: v for k, v in _L0_tok_all.items() if k in ('d_gamma_batched', 'Wq', 'bq', 'Wk', 'bk', 'Wv', 'bv', 'Wo', 'bo', 'prelu_a')}
    del _L0_tok_all

    def _L0_attn_setup():
        import jax, jax.numpy as jnp
        import numpy as np
        B, N, C, H = (1024, 64, 64, 8)
        key = jax.random.key(seed)
        ks = jax.random.split(key, 6)
        return {'x': jax.random.normal(ks[0], (B, N, C), dtype=jnp.float32), 'qkv_w': jax.random.normal(ks[1], (C, 3 * C), dtype=jnp.float32) * 0.02, 'qkv_b': jax.random.normal(ks[2], (3 * C,), dtype=jnp.float32) * 0.02, 'proj_w': jax.random.normal(ks[3], (C, C), dtype=jnp.float32) * 0.02, 'proj_b': jax.random.normal(ks[4], (C,), dtype=jnp.float32) * 0.02, 'rpb_table': jax.random.normal(ks[5], (2 * N - 1, H), dtype=jnp.float32) * 0.02}
    _L0_attn_all = _L0_attn_setup()
    _L0_attn_in = {k: v for k, v in _L0_attn_all.items() if k in ('qkv_w', 'qkv_b', 'proj_w', 'proj_b', 'rpb_table')}
    del _L0_attn_all

    def _L0_ffn_setup():
        import jax, jax.numpy as jnp
        import numpy as np
        E = 8
        K = 2
        D = 64
        H = 128
        DOUT = 64
        EPS = 1e-05
        key = jax.random.key(seed)
        ks = jax.random.split(key, 9)
        s = 0.02
        return {'x': jax.random.normal(ks[0], (4, 2048, D), jnp.float32), 'gamma': 1.0 + 0.05 * jax.random.normal(ks[1], (D,), jnp.float32), 'beta': 0.05 * jax.random.normal(ks[2], (D,), jnp.float32), 'Wr': 0.01 * jax.random.normal(ks[3], (D, E), jnp.float32), 'br': jnp.zeros((E,), jnp.float32), 'W1': s * jax.random.normal(ks[4], (E, D, H), jnp.float32), 'b1': s * jax.random.normal(ks[5], (E, H), jnp.float32), 'W2': s * jax.random.normal(ks[6], (E, H, DOUT), jnp.float32), 'b2': s * jax.random.normal(ks[7], (E, DOUT), jnp.float32)}
    _L0_ffn_all = _L0_ffn_setup()
    _L0_ffn_in = {k: v for k, v in _L0_ffn_all.items() if k in ('gamma', 'beta', 'Wr', 'br', 'W1', 'b1', 'W2', 'b2')}
    del _L0_ffn_all
    return {'x': x, 'L0_tok_d_gamma_batched': _L0_tok_in['d_gamma_batched'], 'L0_tok_Wq': _L0_tok_in['Wq'], 'L0_tok_bq': _L0_tok_in['bq'], 'L0_tok_Wk': _L0_tok_in['Wk'], 'L0_tok_bk': _L0_tok_in['bk'], 'L0_tok_Wv': _L0_tok_in['Wv'], 'L0_tok_bv': _L0_tok_in['bv'], 'L0_tok_Wo': _L0_tok_in['Wo'], 'L0_tok_bo': _L0_tok_in['bo'], 'L0_tok_prelu_a': _L0_tok_in['prelu_a'], 'L0_attn_qkv_w': _L0_attn_in['qkv_w'], 'L0_attn_qkv_b': _L0_attn_in['qkv_b'], 'L0_attn_proj_w': _L0_attn_in['proj_w'], 'L0_attn_proj_b': _L0_attn_in['proj_b'], 'L0_attn_rpb_table': _L0_attn_in['rpb_table'], 'L0_ffn_gamma': _L0_ffn_in['gamma'], 'L0_ffn_beta': _L0_ffn_in['beta'], 'L0_ffn_Wr': _L0_ffn_in['Wr'], 'L0_ffn_br': _L0_ffn_in['br'], 'L0_ffn_W1': _L0_ffn_in['W1'], 'L0_ffn_b1': _L0_ffn_in['b1'], 'L0_ffn_W2': _L0_ffn_in['W2'], 'L0_ffn_b2': _L0_ffn_in['b2']}

def reference(x, L0_tok_d_gamma_batched, L0_tok_Wq, L0_tok_bq, L0_tok_Wk, L0_tok_bk, L0_tok_Wv, L0_tok_bv, L0_tok_Wo, L0_tok_bo, L0_tok_prelu_a, L0_attn_qkv_w, L0_attn_qkv_b, L0_attn_proj_w, L0_attn_proj_b, L0_attn_rpb_table, L0_ffn_gamma, L0_ffn_beta, L0_ffn_Wr, L0_ffn_br, L0_ffn_W1, L0_ffn_b1, L0_ffn_W2, L0_ffn_b2):
    import jax
    import jax.numpy as jnp

    def _L0_tok_ref(x_batched, d_gamma_batched, Wq, bq, Wk, bk, Wv, bv, Wo, bo, prelu_a):
        import jax, jax.numpy as jnp
        import numpy as np
        T, D_IN, D_INT, D_OUT, B = (1024, 64, 64, 64, 8)
        x = x_batched.reshape(x_batched.shape[0], T, D_IN)
        q = x @ Wq + bq
        k = x @ Wk + bk
        v = x @ Wv + bv
        scores = jnp.einsum('btd,bsd->bts', q, k)
        retained = jnp.einsum('bts,bsd->btd', d_gamma_batched * scores, v)
        y = retained @ Wo + bo
        out = jnp.where(y >= 0, y, prelu_a * y)
        return out

    def _L0_attn_ref(x, qkv_w, qkv_b, proj_w, proj_b, rpb_table):
        import jax, jax.numpy as jnp
        import numpy as np
        B, N, C, H = (1024, 64, 64, 8)
        Bw, Nw, Cd = x.shape
        nh = rpb_table.shape[1]
        dh = Cd // nh
        scale = dh ** (-0.5)
        qkv = (x @ qkv_w + qkv_b).reshape(Bw, Nw, 3, nh, dh)
        q, k, v = (qkv[:, :, 0], qkv[:, :, 1], qkv[:, :, 2])
        attn = jnp.einsum('bnhd,bmhd->bhnm', q * scale, k)
        coords = jnp.arange(Nw)
        rel_idx = coords[:, None] - coords[None, :] + (Nw - 1)
        bias = jnp.transpose(rpb_table[rel_idx], (2, 0, 1))
        attn = jax.nn.softmax(attn + bias[None], axis=-1)
        out = jnp.einsum('bhnm,bmhd->bnhd', attn, v).reshape(Bw, Nw, Cd)
        return out @ proj_w + proj_b

    def _L0_ffn_ref(x, gamma, beta, Wr, br, W1, b1, W2, b2):
        import jax, jax.numpy as jnp
        import numpy as np
        E = 8
        K = 2
        D = 64
        H = 128
        DOUT = 64
        EPS = 1e-05
        mu = jnp.mean(x, axis=-1, keepdims=True)
        var = jnp.mean(jnp.square(x - mu), axis=-1, keepdims=True)
        xn = (x - mu) * jax.lax.rsqrt(var + EPS) * gamma + beta
        logits = jnp.einsum('bsd,de->bse', xn, Wr) + br
        top_vals, top_idx = jax.lax.top_k(logits, K)
        w = jax.nn.softmax(top_vals, axis=-1)
        w_full = jnp.einsum('bsk,bske->bse', w, jax.nn.one_hot(top_idx, E, dtype=w.dtype))
        y = jnp.zeros(x.shape[:-1] + (DOUT,), x.dtype)
        for e in range(E):
            h = jax.nn.gelu(jnp.einsum('bsd,dh->bsh', xn, W1[e]) + b1[e], approximate=False)
            y_e = jnp.einsum('bsh,hd->bsd', h, W2[e]) + b2[e]
            y = y + y_e * w_full[..., e, None]
        return y
    h = _L0_tok_ref(x, L0_tok_d_gamma_batched, L0_tok_Wq, L0_tok_bq, L0_tok_Wk, L0_tok_bk, L0_tok_Wv, L0_tok_bv, L0_tok_Wo, L0_tok_bo, L0_tok_prelu_a)
    h = h + _L0_attn_ref(_layernorm(h, axis=-1), L0_attn_qkv_w, L0_attn_qkv_b, L0_attn_proj_w, L0_attn_proj_b, L0_attn_rpb_table)
    h = h + _L0_ffn_ref(_layernorm(h, axis=-1), L0_ffn_gamma, L0_ffn_beta, L0_ffn_Wr, L0_ffn_br, L0_ffn_W1, L0_ffn_b1, L0_ffn_W2, L0_ffn_b2)
    return h

_drawn_inputs = setup_inputs


def setup_inputs(seed=0):
    import zlib

    import numpy as np

    out = dict(_drawn_inputs(seed))
    spreads = {'L0_ffn_br': (0.0, 0.8)}
    factors = {'L0_tok_bo': 34.095,
     'L0_attn_qkv_w': 25.08,
     'L0_attn_qkv_b': 64.0,
     'L0_attn_proj_w': 23.877,
     'L0_attn_proj_b': 64.0,
     'L0_attn_rpb_table': 200.0,
     'L0_ffn_gamma': 8.0,
     'L0_ffn_beta': 21.542,
     'L0_ffn_Wr': 8.0,
     'L0_ffn_W1': 8.0,
     'L0_ffn_b1': 64.0,
     'L0_ffn_W2': 8.0,
     'L0_ffn_b2': 64.0}
    for name, (base, spread) in spreads.items():
        noise = np.random.default_rng([zlib.crc32(name.encode()), seed]).standard_normal(out[name].shape)
        drawn = base * np.exp(spread * noise) if base else spread * noise
        out[name] = jnp.asarray(drawn.astype(out[name].dtype))
    for name, factor in factors.items():
        out[name] = (out[name] * factor).astype(out[name].dtype)
    return out
```

```python
import numpy as np

import concourse.bass as bass
from concourse import mybir
from contextlib import ExitStack



def vit_tower_kernel(nc, x_t, gamma_t, wq, bq, wk, bk, wv, bv, wo, bo, prelu_a, qkv_w, qkv_b, proj_w, proj_b,
                     rpb_rev, ffn_gamma, ffn_beta, wr, br, w1, b1, w2, b2, out):
    fp32 = mybir.dt.float32
    bf16 = mybir.dt.bfloat16
    ALU = mybir.AluOpType
    ACT = mybir.ActivationFunctionType
    AX = mybir.AxisListType.X

    P = 128
    D, N_ALL = x_t.shape
    T = gamma_t.shape[0]
    B = N_ALL // T
    NT = T // P
    HALF = T // 2
    NH, RPB = rpb_rev.shape
    DH = D // NH
    G = B * NH
    E, HID = b1.shape
    PARTS = 3
    TERMS = PARTS * PARTS * DH
    MAXROW = 96
    RING = 4
    VC = 32
    FW = 2 * P
    CH = 512
    NCH = N_ALL // CH
    EPS = 1e-5
    SCALE = float(DH) ** -0.5
    LOWEST = -3.0e38
    ds = bass.ds

    qk_scratch = nc.dram_tensor("qk_parts", [PARTS, 2, G * DH, T], bf16).ap()
    v_scratch = nc.dram_tensor("v_padded", [G, P, NT * VC], fp32).ap()
    f_scratch = nc.dram_tensor("bias_parts", [G, PARTS, FW], bf16).ap()
    out_v = out.rearrange("(n p) d -> p n d", p=P)

    ctx = ExitStack()
    with ctx:
        def sb(name, shape, dt):
            return ctx.enter_context(nc.sbuf_tensor(name, shape, dt))

        def sem(name):
            return ctx.enter_context(nc.semaphore(name))

        gamma_sb = sb("gamma_sb", [P, NT, T], fp32)
        xb = sb("xb", [D + 1, T], fp32)
        wq_a = sb("wq_a", [D + 1, D], fp32)
        wk_a = sb("wk_a", [D + 1, D], fp32)
        wv_a = sb("wv_a", [D + 1, D], fp32)
        wo2 = sb("wo2", [P, D], fp32)
        bo_b = sb("bo_b", [P, D], fp32)
        alpha = sb("alpha", [P, 1], fp32)
        qkv_a = sb("qkv_a", [D + 1, 3 * D], fp32)
        proj_a = sb("proj_a", [D + 1, D], fp32)
        gam_c = sb("gam_c", [D, 1], fp32)
        bet_c = sb("bet_c", [D, 1], fp32)
        wr_a = sb("wr_a", [D + 1, E], fp32)
        w1_a = sb("w1_a", [D + 1, E, HID], fp32)
        w2_s = sb("w2_s", [HID, E, D], fp32)
        b2_r = sb("b2_r", [PARTS * E, D], fp32)
        b2_rest = sb("b2_rest", [PARTS * E, D], fp32)
        b2_p = sb("b2_p", [P, PARTS, D], bf16)
        rpb_s = sb("rpb_s", [NH, RPB], fp32)
        f_diff = sb("f_diff", [NH, FW], fp32)
        f_rest = sb("f_rest", [NH, FW], fp32)
        f_p = sb("f_p", [NH, PARTS, FW], bf16)
        ident = sb("ident", [P, P], fp32)
        ident_b = sb("ident_b", [P, P], bf16)
        flip_b = sb("flip_b", [P, P], bf16)
        pair_sum = sb("pair_sum", [P, D], fp32)
        pick = sb("pick", [P, E, HID], bf16)
        rank = sb("rank", [P, NT, E], fp32)
        ones_done = sb("ones_done", [P, 1], fp32)
        mark = sb("mark", [P, 1], fp32)
        inv_d = sb("inv_d", [P, NT], fp32)
        eps_s = sb("eps_s", [P, NT], fp32)
        zeros = sb("zeros", [P, NT], fp32)
        half_pow = sb("half_pow", [P, NT], fp32)
        qk_scale = sb("qk_scale", [P, 1], fp32)

        q_t = sb("q_t", [D, T], fp32)
        k_t = sb("k_t", [D, T], fp32)
        v_s = sb("v_s", [P, NT, D], fp32)
        gated = sb("gated", [P, 4, HALF], fp32)
        ret_t = sb("ret_t", [P, HALF], fp32)
        y_s = sb("y_s", [P, NT, D], fp32)
        neg_s = sb("neg_s", [P, NT, D], fp32)
        h_all = sb("h_all", [P, B * NT, D], fp32)

        xc = sb("xc", [P, NT, D], fp32)
        sq = sb("sq", [P, NT, D], fp32)
        hn = sb("hn", [P, NT, D], fp32)
        mean = sb("mean", [P, NT], fp32)
        nmean = sb("nmean", [P, NT], fp32)
        var = sb("var", [P, NT], fp32)
        varm = sb("varm", [P, NT], fp32)
        vare = sb("vare", [P, NT], fp32)
        rstd = sb("rstd", [P, NT], fp32)
        hn_t = sb("hn_t", [D + 1, T], fp32)
        qk_h = sb("qk_h", [P, T], bf16)
        qk_rest = sb("qk_rest", [P, T], fp32)
        qk_m = sb("qk_m", [P, T], bf16)
        qk_l = sb("qk_l", [P, T], bf16)
        v_pad = sb("v_pad", [P, NH, NT, VC], fp32)

        q_ring = sb("q_ring", [P, RING, T], bf16)
        k_ring = sb("k_ring", [P, RING, T], bf16)
        x_ring = sb("x_ring", [P, RING, PARTS, P], bf16)
        v_ring = sb("v_ring", [P, RING, NT, VC], fp32)
        probs = sb("probs", [P, 4, T], fp32)
        nmax = sb("nmax", [P, 2, NT], fp32)
        max_rest = sb("max_rest", [P, 2, NT], fp32)
        max_p = sb("max_p", [P, 2, PARTS, NT], bf16)
        max_t = sb("max_t", [PARTS * NT, P], bf16)
        o_t = sb("o_t", [P, 2 * P], fp32)
        o_rec = sb("o_rec", [P, NT], fp32)
        attn = sb("attn", [P, G + 1, NT, DH], fp32)

        ao = sb("ao", [P, NT, D], fp32)
        ao_t = sb("ao_t", [D + 1, T], fp32)
        xn_b = sb("xn_b", [D + 1, T], fp32)
        lg = sb("lg", [P, NT, E], fp32)
        lg2 = sb("lg2", [P, NT, E], fp32)
        eq = sb("eq", [P, NT, E], fp32)
        hot1 = sb("hot1", [P, NT, E], fp32)
        hot2 = sb("hot2", [P, NT, E], fp32)
        top1 = sb("top1", [P, NT], fp32)
        top2 = sb("top2", [P, NT], fp32)
        rk = sb("rk", [P, NT], fp32)
        gap = sb("gap", [P, NT], fp32)
        e_gap = sb("e_gap", [P, NT], fp32)
        den = sb("den", [P, NT], fp32)
        w_top1 = sb("w_top1", [P, NT], fp32)
        w_top2 = sb("w_top2", [P, NT], fp32)
        w_full = sb("w_full", [P, NT, E], fp32)
        w_rest = sb("w_rest", [P, NT, E], fp32)
        w_p = sb("w_p", [P, NT, PARTS, E], bf16)
        xn_all = gamma_sb[0:D + 1, 0:N_ALL // T, :].rearrange("p b t -> p (b t)")
        wt_all = gamma_sb[:, NT // 2:NT // 2 + N_ALL // (2 * T), :].rearrange("p b t -> p (b t)").bitcast(bf16)
        hid = sb("hid", [P, 2, 2 * CH], fp32)
        hid_w = sb("hid_w", [P, 4, CH], fp32)
        ye_t = sb("ye_t", [P, CH], fp32)
        out_s = sb("out_s", [P, 2, CH // P, D], fp32)

        ps = ctx.enter_context(nc.psum_tensor("ps", [P, 8, 512], fp32))

        w_loaded = sem("w_loaded")
        x_loaded = sem("x_loaded")
        gamma_loaded = sem("gamma_loaded")
        pool_seq = sem("pool_seq")
        dve_seq = sem("dve_seq")
        act_seq = sem("act_seq")
        consts_ready = sem("consts_ready")
        zeroed = sem("zeroed")
        pads_ready = sem("pads_ready")
        f_ready = sem("f_ready")
        b2_ready = sem("b2_ready")
        f_stored = sem("f_stored")
        q_projected = sem("q_projected")
        k_projected = sem("k_projected")
        v_projected = sem("v_projected")
        q_copied = sem("q_copied")
        k_copied = sem("k_copied")
        v_copied = sem("v_copied")
        tok_scored = sem("tok_scored")
        tok_gated = sem("tok_gated")
        tok_summed = [sem(f"tok_summed{i}") for i in range(4)]
        ret_copied = sem("ret_copied")
        y_ready = sem("y_ready")
        h_ready = sem("h_ready")

        xc_ready = sem("xc_ready")
        sq_ready = sem("sq_ready")
        var_ready = sem("var_ready")
        vare_ready = sem("vare_ready")
        rstd_ready = sem("rstd_ready")
        hn_ready = sem("hn_ready")
        hn_turned = sem("hn_turned")
        hn_t_copied = sem("hn_t_copied")
        qk_done = sem("qk_done")
        vv_done = sem("vv_done")
        qk_h_ready = sem("qk_h_ready")
        qk_r_ready = sem("qk_r_ready")
        qk_m_ready = sem("qk_m_ready")
        qk_l_ready = sem("qk_l_ready")
        v_pad_ready = sem("v_pad_ready")
        qk_stored = sem("qk_stored")
        v_stored = sem("v_stored")

        operands = [sem(f"operands{u}") for u in range(RING)]
        max_rows = [sem(f"max_rows{u}") for u in range(RING)]
        s1_ready = sem("s1_ready")
        s1_reduced = [sem(f"s1_reduced{i}") for i in range(2)]
        max_seq = sem("max_seq")
        max_split = sem("max_split")
        max_turned = [sem(f"max_turned{i}") for i in range(2)]
        max_copied = sem("max_copied")
        s2_ready = sem("s2_ready")
        exp_done = [sem(f"exp_done{i}") for i in range(2)]
        pv_done = [sem(f"pv_done{i}") for i in range(4)]
        o_copied = [sem(f"o_copied{u}") for u in range(RING)]
        o_turned = sem("o_turned")
        o_normed = sem("o_normed")

        wt_cleared = sem("wt_cleared")
        ao_ready = sem("ao_ready")
        ao_turned = sem("ao_turned")
        ao_t_copied = sem("ao_t_copied")
        proj_done = sem("proj_done")
        xn_turned = sem("xn_turned")
        xn_ready = sem("xn_ready")
        xn_kept = sem("xn_kept")
        routed = sem("routed")
        gap_ready = sem("gap_ready")
        e_gap_ready = sem("e_gap_ready")
        w_split = sem("w_split")
        w_turned = sem("w_turned")
        w_t_copied = sem("w_t_copied")

        up_done = sem("up_done")
        hid_ready = [sem(f"hid_ready{i}") for i in range(2)]
        spread_done = sem("spread_done")
        hid_scaled = [sem(f"hid_scaled{i}") for i in range(4)]
        down_done = [sem(f"down_done{i}") for i in range(4)]
        ye_copied = sem("ye_copied")
        ffn_done = sem("ffn_done")
        out_ready = sem("out_ready")
        route_seq = sem("route_seq")
        res_seq = sem("res_seq")
        rec_ready = sem("rec_ready")
        norm_seq = sem("norm_seq")
        y_seq = sem("y_seq")
        out_stored = [sem(f"out_stored{i}") for i in range(2)]

        N_W_LOADS = 25
        N_OPERANDS = 2 * PARTS + 2
        ROUTE_STEPS = 21
        S1A, S2A, PVB, MISC = 0, 4, 6, 7
        max_ps = ps[:, MISC, :].bitcast(bf16)[0:PARTS * NT, 4 * P:5 * P]

        block = ctx.enter_context(nc.Block())

        @block.sync
        def _(sp):
            def load(dst, src):
                sp.dma_start(dst, src).then_inc(w_loaded, 16)

            row = lambda v: v.rearrange("(a n) -> a n", a=1)
            col = lambda v: v.rearrange("(n a) -> n a", a=1)
            load(wq_a[0:D, :], wq)
            load(wq_a[D:D + 1, :], row(bq))
            load(wk_a[0:D, :], wk)
            load(wk_a[D:D + 1, :], row(bk))
            load(wv_a[0:D, :], wv)
            load(wv_a[D:D + 1, :], row(bv))
            load(wo2[0:D, :], wo)
            load(wo2[D:2 * D, :], wo)
            load(bo_b[:, :], row(bo).to_broadcast([P, D]))
            load(alpha[:, :], prelu_a.to_broadcast([P, 1]))
            load(rpb_s[:, :], rpb_rev)
            for i in range(PARTS):
                load(b2_r[E * i:E * i + E, :], b2)
            load(qkv_a[0:D, :], qkv_w)
            load(qkv_a[D:D + 1, :], row(qkv_b))
            load(proj_a[0:D, :], proj_w)
            load(proj_a[D:D + 1, :], row(proj_b))
            load(gam_c[:, :], col(ffn_gamma))
            load(bet_c[:, :], col(ffn_beta))
            load(wr_a[0:D, :], wr)
            load(wr_a[D:D + 1, :], row(br))
            load(w1_a[0:D, :, :], w1.rearrange("e d h -> d e h"))
            load(w1_a[D:D + 1, :, :], b1.rearrange("(a e) h -> a e h", a=1))
            load(w2_s[:, :, :], w2.rearrange("e h d -> h e d"))

            gamma_v = gamma_t.rearrange("(s p) t -> p s t", p=P)
            for j in range(2):
                m = slice(NT // 2 * j, NT // 2 * (j + 1))
                sp.dma_start(gamma_sb[:, m, :], gamma_v[:, m, :]).then_inc(gamma_loaded, 16)

            with sp.Fori(0, B) as b:
                sp.wait_ge(v_projected, b)
                sp.dma_start(xb[0:D, :], x_t[:, ds(b * T, T)]).then_inc(x_loaded, 16)

            sp.wait_ge(f_ready, 1)
            for b in range(B):
                sp.dma_start(f_scratch[NH * b:NH * b + NH, :, :], f_p[:, :, :]).then_inc(f_stored, 16)

            with sp.Fori(0, B) as b:
                def store_parts(i, parts):
                    for qk in range(2):
                        sp.dma_start(qk_scratch[i, qk, ds(b * D, D), :],
                                     parts[D * qk:D * qk + D, :]).then_inc(qk_stored, 16)

                sp.wait_ge(qk_h_ready, b + 1)
                store_parts(0, qk_h)
                sp.wait_ge(v_pad_ready, b + 1)
                sp.dma_start(v_scratch[ds(b * NH, NH), :, :].rearrange("h p n -> p h n"),
                             v_pad[:, :, :, :].rearrange("p h m c -> p h (m c)")).then_inc(v_stored, 16)
                sp.wait_ge(qk_m_ready, b + 1)
                store_parts(1, qk_m)
                sp.wait_ge(qk_l_ready, b + 1)
                store_parts(2, qk_l)

            sp.wait_ge(f_stored, 16 * B)
            sp.wait_ge(qk_stored, 2 * 16 * PARTS * B)
            sp.wait_ge(v_stored, 16 * B)
            sp.wait_ge(pads_ready, 1)

            def load_head(g, u):
                rows = PARTS * DH
                for i in range(PARTS):
                    q_i = qk_scratch[i, 0, ds(g * DH, DH), :].rearrange("(o d) t -> o d t", o=1)
                    sp.dma_start(q_ring[rows * i:rows * (i + 1), u, :],
                                 q_i.to_broadcast([PARTS, DH, T])).then_inc(operands[u], 16)
                    sp.dma_start(k_ring[rows * i:rows * (i + 1), u, :],
                                 qk_scratch[:, 1, ds(g * DH, DH), :]).then_inc(operands[u], 16)
                f_g = f_scratch[ds(g, 1), :, :]
                sp.dma_start(x_ring[:, u, :, :],
                             bass.AP(tensor=f_g.tensor, offset=f_g.offset, ap=[[1, P], [FW, PARTS], [1, P]])
                             ).then_inc(operands[u], 16)
                sp.dma_start(v_ring[:, u, :, :],
                             v_scratch[ds(g, 1), :, :].rearrange("o p n -> (o p) n")).then_inc(operands[u], 16)

            def send_max_rows(n, u):
                sp.wait_ge(max_copied, n + 1)
                sp.dma_start(q_ring[MAXROW:MAXROW + PARTS, u, :], max_t[:, :]).then_inc(max_rows[u], 16)

            for u in range(RING):
                load_head(u, u)
            send_max_rows(0, 0)
            with sp.Fori(0, G // RING - 1) as it:
                for u in range(RING):
                    send_max_rows(it * RING + (u + 1), (u + 1) % RING)
                    sp.wait_ge(o_copied[u], it + 1)
                    load_head(it * RING + (u + RING), u)
            for u in range(RING - 1):
                send_max_rows(G - RING + u + 1, u + 1)

            with sp.Fori(0, NCH // 2) as c2:
                for i in range(2):
                    sp.wait_ge(out_ready, c2 * 2 + (i + 1))
                    sp.dma_start(out_v[:, ds(c2 * (2 * CH // P) + i * (CH // P), CH // P), :],
                                 out_s[:, i, :, :]).then_inc(out_stored[i], 16)
            for i in range(2):
                sp.wait_ge(out_stored[i], 16 * (NCH // 2))

        @block.gpsimd
        def _(pool):
            seq = [0]

            def after(ins):
                seq[0] += 1
                ins.then_inc(pool_seq, 1)
                pool.wait_ge(pool_seq, seq[0])

            gp = nc.gpsimd
            for m in (ident[:, :], ident_b[:, :], flip_b[:, :], pair_sum[:, :], pick[:, :, :]):
                after(gp.memset(m, 0.0))

            def ones_where(m, base, pattern, mult):
                after(gp.affine_select(out=m, in_=m, compare_op=ALU.not_equal, fill=1.0, base=base,
                                       pattern=pattern, channel_multiplier=mult))

            ones_where(ident[:, :], 0, [[-1, P]], 1)
            ones_where(ident_b[:, :], 0, [[-1, P]], 1)
            ones_where(flip_b[:, :], 1 - P, [[1, P]], 1)
            for e in range(2):
                ones_where(pair_sum[:, :], -D * e, [[-1, D]], 1)
            for i in range(PARTS):
                ones_where(pick[:, :, :], -E * i, [[-1, E], [0, HID]], 1)
            gp.memset(ones_done[:, :], 0.0).then_inc(consts_ready, 1)

            pool.wait_ge(pads_ready, 1)

            def norm_power(n):
                pool.wait_ge(var_ready, n + 1)
                gp.tensor_tensor(varm[:, :], var[:, :], inv_d[:, :], ALU.mult).then_inc(vare_ready, 1)
                pool.wait_ge(vare_ready, n * 2 + 1)
                gp.tensor_tensor(vare[:, :], varm[:, :], eps_s[:, :], ALU.add).then_inc(vare_ready, 1)
                pool.wait_ge(vare_ready, n * 2 + 2)
                gp.tensor_tensor(rstd[:, :], vare[:, :], half_pow[:, :], ALU.pow).then_inc(rstd_ready, 1)

            with pool.Fori(0, B) as b:
                norm_power(b)

            pool.wait_ge(h_ready, B)
            gp.memset(wt_all, 0.0).then_inc(wt_cleared, 1)
            pool.wait_ge(wt_cleared, 1)
            gp.memset(xn_all[D:D + 1, :], 1.0).then_inc(wt_cleared, 1)
            pool.wait_ge(wt_cleared, 2)

            with pool.Fori(0, G // 2) as g2:
                for v in range(2):
                    g = g2 * 2 + v
                    pool.wait_ge(s1_reduced[0], g * (NT // 2) + NT // 2)
                    pool.wait_ge(s1_reduced[1], g * (NT // 2) + NT // 2)
                    pool.wait_ge(max_turned[v], g2)
                    k = g * 3

                    def step(n, ins):
                        ins.then_inc(max_seq, 1)
                        pool.wait_ge(max_seq, k + n)

                    p0, p1, p2 = (max_p[:, v, i, :] for i in range(PARTS))
                    step(1, gp.tensor_tensor(p0, nmax[:, v, :], zeros[:, :], ALU.add))
                    step(2, gp.tensor_tensor(max_rest[:, v, :], nmax[:, v, :], p0, ALU.subtract))
                    step(3, gp.tensor_tensor(p1, max_rest[:, v, :], zeros[:, :], ALU.add))
                    gp.tensor_tensor(p2, max_rest[:, v, :], p1, ALU.subtract).then_inc(max_split, 1)

            with pool.Fori(0, B) as b:
                for i in range(2):
                    norm_power(b * 2 + (B + i))

        @block.scalar
        def _(act):
            A = nc.scalar
            act.wait_ge(pads_ready, 1)

            with act.Fori(0, B) as b:
                for j in range(2):
                    act.wait_ge(q_projected, b * 2 + (j + 1))
                    A.activation(q_t[:, HALF * j:HALF * (j + 1)], ps[0:D, j, :], ACT.Copy).then_inc(q_copied, 1)
                act.wait_ge(v_projected, b + 1)
                A.activation(v_s[:, :, :], ps[:, 4, :].rearrange("p (m d) -> p m d", d=D),
                             ACT.Copy).then_inc(v_copied, 1)
                act.wait_ge(tok_summed[3], b * 4 + 4)
                act.wait_ge(y_ready, b)
                A.activation(ret_t[:, :], ps[:, 5, :], ACT.Copy).then_inc(ret_copied, 1)

            def square(n):
                act.wait_ge(xc_ready, n + 1)
                A.activation(sq[:, :, :], xc[:, :, :], ACT.Square).then_inc(sq_ready, 1)

            with act.Fori(0, B) as b:
                square(b)
                act.wait_ge(hn_turned, b + 1)
                act.wait_ge(vv_done, b)
                A.activation(hn_t[0:D, :], ps[0:D, 0:2, :].rearrange("p a n -> p (a n)"),
                             ACT.Copy).then_inc(hn_t_copied, 1)
                act.wait_ge(qk_done, b + 1)
                act.wait_ge(qk_stored, b * (2 * 16 * PARTS))
                A.activation(qk_h[:, :], ps[:, 2:4, :].rearrange("p a n -> p (a n)"), ACT.Identity,
                             scale=qk_scale[:, 0:1]).then_inc(qk_h_ready, 1)
                act.wait_ge(vv_done, b + 1)
                act.wait_ge(v_stored, b * 16)
                A.activation(v_pad[:, :, :, 0:DH].rearrange("p h m c -> p m h c"),
                             ps[:, 4, :].rearrange("p (m h c) -> p m h c", h=NH, c=DH),
                             ACT.Copy).then_inc(v_pad_ready, 1)
                act.wait_ge(qk_r_ready, b + 1)
                A.activation(qk_m[:, :], qk_rest[:, :], ACT.Copy).then_inc(qk_m_ready, 1)

            def max_rows_copy(turned, par, sent, sent_slot):
                act.wait_ge(max_turned[par], turned)
                if sent is not None:
                    act.wait_ge(max_rows[sent_slot], sent)
                A.activation(max_t[:, :], max_ps, ACT.Copy).then_inc(max_copied, 1)

            def attend_act(it, last):
                for u in range(RING):
                    g = it * RING + u
                    for s in range(NT):
                        for j in range(2):
                            act.wait_ge(s2_ready, g * (2 * NT) + (2 * s + j + 1))
                            if j == 0:
                                act.wait_ge(pv_done[s % 4], g * (NT // 4) + s // 4)
                            A.activation(probs[:, s % 4, HALF * j:HALF * (j + 1)], ps[:, S2A + j, :],
                                         ACT.Exp).then_inc(exp_done[j], 1)
                        if s == 4 and not (last and u == RING - 1):
                            max_rows_copy(it * 2 + ((u + 1) // 2 + 1), (u + 1) % 2, it * 16 + 16, u)
                    act.wait_ge(pv_done[3], g * (NT // 4) + NT // 4)
                    act.wait_ge(o_turned, g + 1)
                    A.activation(o_t[:, :], ps[:, PVB, 0:2 * P], ACT.Copy).then_inc(o_copied[u], 1)

            max_rows_copy(1, 0, None, None)
            with act.Fori(0, G // RING - 1) as it:
                attend_act(it, False)
            attend_act(G // RING - 1, True)

            act.wait_ge(o_normed, G + 1)
            act.wait_ge(wt_cleared, 2)
            with act.Fori(0, B) as b:
                act.wait_ge(ao_turned, b)
                A.activation(ao[:, :, :].rearrange("p m (h c) -> p m h c", c=DH),
                             attn[:, ds(b * NH + 1, NH), :, :].rearrange("p h m c -> p m h c"),
                             ACT.Copy).then_inc(ao_ready, 1)
                act.wait_ge(ao_turned, b + 1)
                act.wait_ge(proj_done, b)
                A.activation(ao_t[0:D, :], ps[0:D, 0:2, :].rearrange("p a n -> p (a n)"),
                             ACT.Copy).then_inc(ao_t_copied, 1)
                for i in range(2):
                    square(b * 2 + (B + i))
                act.wait_ge(xn_ready, b + 1)
                A.activation(xn_all[:, ds(b * T, T)], xn_b[:, :], ACT.Copy).then_inc(xn_kept, 1)
                act.wait_ge(gap_ready, b + 1)
                A.activation(e_gap[:, :], gap[:, :], ACT.Exp).then_inc(e_gap_ready, 1)
                act.wait_ge(w_turned, b + 1)
                A.activation(wt_all[0:PARTS * E, ds(b * T, T)], ps[:, 4, :].bitcast(bf16)[0:PARTS * E, 0:T],
                             ACT.Copy).then_inc(w_t_copied, 1)

            with act.Fori(0, NCH // 2) as c2:
                for i in range(2):
                    n = c2 * 2 + i
                    for e2 in range(E // 2):
                        act.wait_ge(up_done, n * (E // 2) + (e2 + 1))
                        act.wait_ge(hid_scaled[(2 * e2 - 3) % 4], n * 2 + e2 // 2)
                        A.activation(hid[:, e2 % 2, :],
                                     ps[:, 2 * (e2 % 2):2 * (e2 % 2) + 2, :].rearrange("p a n -> p (a n)"),
                                     ACT.Gelu).then_inc(hid_ready[e2 % 2], 1)
                    for k in (2, 3):
                        act.wait_ge(down_done[k], n * 2 + 2)
                    act.wait_ge(ffn_done, n)
                    A.activation(ye_t[:, :], ps[:, 6, :], ACT.Copy).then_inc(ye_copied, 1)

        @block.vector
        def _(dve):
            V = nc.vector

            def chain(counter, base):
                count = [0]

                def step(ins):
                    count[0] += 1
                    ins.then_inc(counter, 1)
                    dve.wait_ge(counter, base + count[0])
                return step

            V.memset(v_pad[:, :, :, :], 0.0)
            V.memset(q_ring[D:P, :, :], 0.0)
            V.memset(k_ring[D:P, :, :], 0.0)
            V.memset(b2_p[:, :, :], 0.0)
            V.memset(f_diff[:, :], 0.0).then_inc(zeroed, 1)
            dve.wait_ge(zeroed, 1)
            V.memset(v_pad[:, :, :, DH:DH + 1], 1.0)
            V.memset(k_ring[MAXROW:MAXROW + PARTS, :, :], 1.0)
            for e in range(E):
                V.memset(rank[:, :, e:e + 1], float(E - e))
            for m, value in ((half_pow, -0.5), (inv_d, 1.0 / D), (eps_s, EPS), (zeros, 0.0), (o_t, 1.0)):
                V.memset(m[:, :], value)
            V.memset(qk_scale[0:D, :], SCALE)
            V.memset(qk_scale[D:P, :], 1.0)
            for aug in (xb, hn_t, ao_t, xn_b):
                V.memset(aug[D:D + 1, :], 1.0)
            V.memset(mark[:, :], 0.0).then_inc(pads_ready, 1)

            dve.wait_ge(w_loaded, 16 * N_W_LOADS)
            dve.wait_ge(pads_ready, 1)
            step = chain(dve_seq, 0)
            step(V.tensor_scalar(f_diff[:, P:P + RPB], rpb_s[:, :], rpb_s[:, 0:1], None, ALU.subtract))
            step(V.tensor_copy(f_p[:, 0, :], f_diff[:, :]))
            step(V.tensor_tensor(f_rest[:, :], f_diff[:, :], f_p[:, 0, :], ALU.subtract))
            step(V.tensor_copy(f_p[:, 1, :], f_rest[:, :]))
            V.tensor_tensor(f_p[:, 2, :], f_rest[:, :], f_p[:, 1, :], ALU.subtract).then_inc(f_ready, 1)
            rows = slice(0, PARTS * E)
            step(V.tensor_copy(b2_p[rows, 0, :], b2_r[:, :]))
            step(V.tensor_tensor(b2_rest[:, :], b2_r[:, :], b2_p[rows, 0, :], ALU.subtract))
            step(V.tensor_copy(b2_p[rows, 1, :], b2_rest[:, :]))
            V.tensor_tensor(b2_p[rows, 2, :], b2_rest[:, :], b2_p[rows, 1, :], ALU.subtract).then_inc(b2_ready, 1)
            dve.wait_ge(gamma_loaded, 16 * 2)

            with dve.Fori(0, B) as b:
                for j in range(2):
                    dve.wait_ge(k_projected, b * 2 + (j + 1))
                    V.tensor_copy(k_t[:, HALF * j:HALF * (j + 1)], ps[0:D, 2 + j, :]).then_inc(k_copied, 1)
                for u in range(2 * NT):
                    s, j = u // 2, u % 2
                    dve.wait_ge(tok_scored, b * (2 * NT) + (u + 1))
                    dve.wait_ge(tok_summed[u % 4], b * (2 * NT // 4) + u // 4)
                    V.tensor_tensor(gated[:, u % 4, :], ps[:, u % 4, :],
                                    gamma_sb[:, s, HALF * j:HALF * (j + 1)], ALU.mult).then_inc(tok_gated, 1)
                dve.wait_ge(y_ready, b + 1)
                step = chain(y_seq, b * 3)
                for j in range(2):
                    m = slice(NT // 2 * j, NT // 2 * (j + 1))
                    bo_m = bo_b[:, :].rearrange("p (o d) -> p o d", o=1).to_broadcast([P, NT // 2, D])
                    step(V.tensor_tensor(y_s[:, m, :], ps[:, 6 + j, 0:NT // 2 * D].rearrange("p (m d) -> p m d", d=D),
                                         bo_m, ALU.add))
                step(V.tensor_scalar(neg_s[:, :, :], y_s[:, :, :], 0.0, alpha[:, 0:1], ALU.min, ALU.mult))
                V.scalar_tensor_tensor(out=h_all[:, ds(b * NT, NT), :], in0=y_s[:, :, :], scalar=0.0,
                                       in1=neg_s[:, :, :], op0=ALU.max, op1=ALU.add).then_inc(h_ready, 1)

            def over_d(m):
                return m[:, :].rearrange("p (m o) -> p m o", o=1).to_broadcast([P, NT, D])

            def layer_norm(src, n, counter):
                step = chain(counter, n * 2)
                V.memset(mark[:, :], 0.0)
                step(V.tensor_reduce(mean[:, :], src, AX, ALU.add))
                step(V.tensor_scalar(nmean[:, :], mean[:, :], -1.0 / D, None, ALU.mult))
                V.tensor_tensor(xc[:, :, :], src, over_d(nmean), ALU.add).then_inc(xc_ready, 1)
                dve.wait_ge(sq_ready, n + 1)
                V.tensor_reduce(var[:, :], sq[:, :, :], AX, ALU.add).then_inc(var_ready, 1)
                dve.wait_ge(rstd_ready, n + 1)
                dve.wait_ge(xc_ready, n + 1)
                V.tensor_tensor(hn[:, :, :], xc[:, :, :], over_d(rstd), ALU.mult).then_inc(hn_ready, 1)

            with dve.Fori(0, B) as b:
                dve.wait_ge(h_ready, b + 1)
                dve.wait_ge(hn_turned, b)
                layer_norm(h_all[:, ds(b * NT, NT), :], b, norm_seq)
                dve.wait_ge(qk_done, b + 1)
                dve.wait_ge(qk_h_ready, b + 1)
                dve.wait_ge(qk_m_ready, b)
                V.scalar_tensor_tensor(out=qk_rest[:, :], in0=ps[:, 2:4, :].rearrange("p a n -> p (a n)"),
                                       scalar=qk_scale[:, 0:1], in1=qk_h[:, :], op0=ALU.mult,
                                       op1=ALU.subtract).then_inc(qk_r_ready, 1)
                dve.wait_ge(qk_r_ready, b + 1)
                dve.wait_ge(qk_m_ready, b + 1)
                dve.wait_ge(qk_stored, b * (2 * 16 * PARTS))
                V.tensor_tensor(qk_l[:, :], qk_rest[:, :], qk_m[:, :], ALU.subtract).then_inc(qk_l_ready, 1)

            def row_max(g, s, par):
                dve.wait_ge(s1_ready, g * NT + (s + 1))
                bank = S1A + 2 * (s % 2)
                V.tensor_reduce(nmax[:, par, s:s + 1], ps[:, bank:bank + 2, :].rearrange("p a n -> p (a n)"),
                                AX, ALU.max, negate=True).then_inc(s1_reduced[s % 2], 1)

            def normalize(n):
                dve.wait_ge(o_turned, n + 1)
                o_v = ps[:, MISC, 0:2 * P].rearrange("p (c j x) -> p c j x", c=2, x=VC)
                rec_v = o_rec[:, :].rearrange("p (c j o) -> p c j o", c=2, o=1)
                V.reciprocal(rec_v, o_v[:, :, :, DH:DH + 1]).then_inc(rec_ready, 1)
                dve.wait_ge(rec_ready, n + 1)
                V.tensor_tensor(attn[:, ds(n, 1), :, :].rearrange("p a (j c) d -> p (a c) j d", c=2),
                                o_v[:, :, :, 0:DH], rec_v.to_broadcast([P, 2, NT // 2, DH]),
                                ALU.mult).then_inc(o_normed, 1)

            for g in range(2):
                for s in range(NT):
                    row_max(g, s, g)

            def attend_dve(it, last):
                for u in range(RING):
                    g = it * RING + u
                    for s in range(NT):
                        if not (last and u >= RING - 2):
                            if s == 0:
                                dve.wait_ge(max_split, g + 1)
                            row_max(g + 2, s, u % 2)
                        if s == 3:
                            normalize(g)

            with dve.Fori(0, G // RING - 1) as it:
                attend_dve(it, False)
            attend_dve(G // RING - 1, True)
            normalize(G)

            with dve.Fori(0, B) as b:
                h_b = h_all[:, ds(b * NT, NT), :]
                dve.wait_ge(proj_done, b + 1)
                V.tensor_tensor(h_b, h_b, ps[:, 2, :].rearrange("p (m d) -> p m d", d=D), ALU.add).then_inc(res_seq, 1)
                dve.wait_ge(res_seq, b + 1)
                dve.wait_ge(xn_turned, b)
                layer_norm(h_b, b * 2 + B, norm_seq)
                dve.wait_ge(hn_ready, b * 2 + (B + 1))
                layer_norm(hn[:, :, :], b * 2 + (B + 1), norm_seq)
                dve.wait_ge(xn_turned, b + 1)
                dve.wait_ge(xn_kept, b)
                V.tensor_scalar(xn_b[0:D, :], ps[0:D, 0:2, :].rearrange("p a n -> p (a n)"), gam_c[:, 0:1],
                                bet_c[:, 0:1], ALU.mult, ALU.add).then_inc(xn_ready, 1)
                dve.wait_ge(routed, b + 1)

                def over_e(m):
                    return m[:, :].rearrange("p (m o) -> p m o", o=1).to_broadcast([P, NT, E])

                step = chain(route_seq, b * ROUTE_STEPS)
                step(V.tensor_copy(lg[:, :, :], ps[:, 3, 0:NT * E].rearrange("p (m e) -> p m e", e=E)))
                step(V.tensor_reduce(top1[:, :], lg[:, :, :], AX, ALU.max))
                step(V.tensor_tensor(eq[:, :, :], lg[:, :, :], over_e(top1), ALU.is_equal))
                step(V.tensor_tensor(eq[:, :, :], eq[:, :, :], rank[:, :, :], ALU.mult))
                step(V.tensor_reduce(rk[:, :], eq[:, :, :], AX, ALU.max))
                step(V.tensor_tensor(hot1[:, :, :], rank[:, :, :], over_e(rk), ALU.is_equal))
                step(V.scalar_tensor_tensor(out=lg2[:, :, :], in0=hot1[:, :, :], scalar=LOWEST, in1=lg[:, :, :],
                                            op0=ALU.mult, op1=ALU.add))
                step(V.tensor_reduce(top2[:, :], lg2[:, :, :], AX, ALU.max))
                V.tensor_tensor(gap[:, :], top2[:, :], top1[:, :], ALU.subtract).then_inc(gap_ready, 1)
                step(V.tensor_tensor(eq[:, :, :], lg2[:, :, :], over_e(top2), ALU.is_equal))
                step(V.tensor_tensor(eq[:, :, :], eq[:, :, :], rank[:, :, :], ALU.mult))
                step(V.tensor_reduce(rk[:, :], eq[:, :, :], AX, ALU.max))
                step(V.tensor_tensor(hot2[:, :, :], rank[:, :, :], over_e(rk), ALU.is_equal))
                dve.wait_ge(e_gap_ready, b + 1)
                step(V.tensor_scalar(den[:, :], e_gap[:, :], 1.0, None, ALU.add))
                step(V.reciprocal(w_top1[:, :], den[:, :]))
                step(V.tensor_tensor(w_top2[:, :], w_top1[:, :], e_gap[:, :], ALU.mult))
                step(V.tensor_tensor(hot1[:, :, :], hot1[:, :, :], over_e(w_top1), ALU.mult))
                step(V.tensor_tensor(hot2[:, :, :], hot2[:, :, :], over_e(w_top2), ALU.mult))
                step(V.tensor_tensor(w_full[:, :, :], hot1[:, :, :], hot2[:, :, :], ALU.add))
                dve.wait_ge(w_turned, b)
                step(V.tensor_copy(w_p[:, :, 0, :], w_full[:, :, :]))
                step(V.tensor_tensor(w_rest[:, :, :], w_full[:, :, :], w_p[:, :, 0, :], ALU.subtract))
                step(V.tensor_copy(w_p[:, :, 1, :], w_rest[:, :, :]))
                V.tensor_tensor(w_p[:, :, 2, :], w_rest[:, :, :], w_p[:, :, 1, :], ALU.subtract).then_inc(w_split, 1)

            with dve.Fori(0, NCH // 2) as c2:
                for i in range(2):
                    n = c2 * 2 + i
                    for e in range(E):
                        dve.wait_ge(hid_ready[(e // 2) % 2], n * 2 + (e // 4 + 1))
                        dve.wait_ge(spread_done, n * E + (e + 1))
                        dve.wait_ge(down_done[e % 4], n * 2 + e // 4)
                        V.tensor_tensor(hid_w[:, e % 4, :], hid[:, (e // 2) % 2, CH * (e % 2):CH * (e % 2 + 1)],
                                        ps[:, 4 + e % 2, :], ALU.mult).then_inc(hid_scaled[e % 4], 1)
                    dve.wait_ge(ffn_done, n + 1)
                    dve.wait_ge(out_stored[i], c2 * 16)
                    V.tensor_tensor(out_s[:, i, :, :], ps[:, 7, 0:CH // P * D].rearrange("p (m d) -> p m d", d=D),
                                    h_all[:, ds(n * (CH // P), CH // P), :], ALU.add).then_inc(out_ready, 1)

        @block.tensor
        def _(pe):
            mm = nc.tensor.matmul

            pe.wait_ge(w_loaded, 16 * N_W_LOADS)
            pe.wait_ge(consts_ready, 1)
            pe.wait_ge(pads_ready, 1)
            with pe.Fori(0, B) as b:
                pe.wait_ge(x_loaded, b * 16 + 16)
                pe.wait_ge(tok_gated, b * (2 * NT))
                for j in range(2):
                    mm(ps[0:D, j, :], wq_a[:, :], xb[:, HALF * j:HALF * (j + 1)], start=True,
                       stop=True).then_inc(q_projected, 1)
                for j in range(2):
                    mm(ps[0:D, 2 + j, :], wk_a[:, :], xb[:, HALF * j:HALF * (j + 1)], start=True,
                       stop=True).then_inc(k_projected, 1)
                pe.wait_ge(v_copied, b)
                for m in range(NT):
                    last = mm(ps[:, 4, D * m:D * (m + 1)], xb[:, P * m:P * (m + 1)], wv_a[:, :],
                              start=True, stop=True)
                last.then_inc(v_projected, 1)

                def score(u):
                    s, j = u // 2, u % 2
                    if u >= 4:
                        pe.wait_ge(tok_gated, b * (2 * NT) + (u - 3))
                    mm(ps[:, u % 4, :], k_t[:, P * s:P * (s + 1)], q_t[:, HALF * j:HALF * (j + 1)],
                       start=True, stop=True).then_inc(tok_scored, 1)

                def retain(u):
                    s, j = u // 2, u % 2
                    pe.wait_ge(tok_gated, b * (2 * NT) + (u + 1))
                    mm(ps[D * j:D * (j + 1), 5, :], v_s[:, s, :], gated[:, u % 4, :], start=(s == 0),
                       stop=(s == NT - 1)).then_inc(tok_summed[u % 4], 1)

                pe.wait_ge(q_copied, b * 2 + 2)
                pe.wait_ge(k_copied, b * 2 + 2)
                for u in range(2):
                    score(u)
                pe.wait_ge(v_copied, b + 1)
                pe.wait_ge(ret_copied, b)
                for u in range(2 * NT):
                    if u + 2 < 2 * NT:
                        score(u + 2)
                    retain(u)
                pe.wait_ge(ret_copied, b + 1)
                pe.wait_ge(h_ready, b)
                for j in range(2):
                    for m in range(NT // 2):
                        last = mm(ps[:, 6 + j, D * m:D * (m + 1)], ret_t[D * j:D * (j + 1), P * m:P * (m + 1)],
                                  wo2[D * j:D * (j + 1), :], start=True, stop=True)
                last.then_inc(y_ready, 1)

            def turn(src, done):
                mm(ps[:, MISC, 0:1], ident_b[:, :], ident_b[:, 0:1], start=True, stop=True)
                for m in range(NT):
                    c = m % (NT // 2)
                    last = nc.tensor.transpose(ps[0:D, m // (NT // 2), P * c:P * (c + 1)], src[:, m, :], ident[:, :])
                last.then_inc(done, 1)

            with pe.Fori(0, B) as b:
                pe.wait_ge(hn_ready, b + 1)
                pe.wait_ge(hn_t_copied, b)
                turn(hn, hn_turned)
                pe.wait_ge(hn_t_copied, b + 1)
                pe.wait_ge(qk_r_ready, b)
                for j in range(2):
                    last = mm(ps[:, 2 + j, :], qkv_a[:, 0:2 * D], hn_t[:, HALF * j:HALF * (j + 1)],
                              start=True, stop=True)
                last.then_inc(qk_done, 1)
                pe.wait_ge(v_pad_ready, b)
                for m in range(NT):
                    last = mm(ps[:, 4, D * m:D * (m + 1)], hn_t[:, P * m:P * (m + 1)], qkv_a[:, 2 * D:3 * D],
                              start=True, stop=True)
                last.then_inc(vv_done, 1)
            pe.wait_ge(qk_r_ready, B)
            pe.wait_ge(v_pad_ready, B)

            def scores_by_query(g, s, u):
                pe.wait_ge(s1_reduced[s % 2], g * (NT // 2) + s // 2)
                bank = S1A + 2 * (s % 2)
                for j in range(2):
                    last = mm(ps[:, bank + j, :], q_ring[0:MAXROW, u, P * s:P * (s + 1)],
                              k_ring[0:MAXROW, u, HALF * j:HALF * (j + 1)], start=True, stop=(s > 0 or j == 0))
                if s == 0:
                    for i in range(PARTS):
                        last = mm(ps[:, bank + 1, HALF - P:HALF], flip_b[:, :], x_ring[:, u, i, :],
                                  start=False, stop=(i == PARTS - 1))
                last.then_inc(s1_ready, 1)

            def scores_by_key(g, s, u):
                for j in range(2):
                    pe.wait_ge(exp_done[j], g * NT + s)
                    corner = s == NT - 1 and j == 0
                    last = mm(ps[:, S2A + j, :], k_ring[0:MAXROW + PARTS, u, P * s:P * (s + 1)],
                              q_ring[0:MAXROW + PARTS, u, HALF * j:HALF * (j + 1)], start=True, stop=not corner)
                    if corner:
                        for i in range(PARTS):
                            last = mm(ps[:, S2A, 0:P], x_ring[:, u, i, :], flip_b[:, :], start=False,
                                      stop=(i == PARTS - 1))
                    last.then_inc(s2_ready, 1)

            def values(it, g, m, u):
                if m == 0:
                    pe.wait_ge(o_copied[(u - 1) % RING], it + (1 if u else 0))
                for j in range(2):
                    pe.wait_ge(exp_done[j], g * NT + (m + 1))
                for j in range(4):
                    last = mm(ps[VC * j:VC * (j + 1), PVB, 0:2 * P], v_ring[:, u, m, :],
                              probs[:, m % 4, 2 * P * j:2 * P * (j + 1)], start=(m == 0), stop=(m == NT - 1))
                last.then_inc(pv_done[m % 4], 1)

            def turn_output(n, before, copied, final=False):
                pe.wait_ge(o_copied[before], copied)
                pe.wait_ge(max_copied, G if final else n + 1)
                if final:
                    pe.wait_ge(o_normed, G)
                for c in range(2):
                    last = nc.tensor.transpose(ps[:, MISC, P * c:P * (c + 1)], o_t[:, P * c:P * (c + 1)], ident[:, :])
                last.then_inc(o_turned, 1)

            def turn_maxima(g, par):
                pe.wait_ge(max_split, g + 1)
                pe.wait_ge(o_normed, g)
                nc.tensor.transpose(max_ps, max_p[:, par, :, :].rearrange("p a m -> p (a m)"),
                                    ident_b[:, :]).then_inc(max_turned[par], 1)

            for g in range(2):
                pe.wait_ge(operands[g], 16 * N_OPERANDS)
                for s in range(NT):
                    scores_by_query(g, s, g)
            turn_maxima(0, 0)

            def attend_pe(it, last):
                for u in range(RING):
                    g = it * RING + u
                    ahead = not (last and u >= RING - 2)
                    pe.wait_ge(max_rows[u], it * 16 + 16)
                    if ahead:
                        pe.wait_ge(operands[(u + 2) % RING],
                                   (it + (u + 2) // RING) * (16 * N_OPERANDS) + 16 * N_OPERANDS)
                    for s in range(NT):
                        scores_by_key(g, s, u)
                        if ahead:
                            scores_by_query(g + 2, s, (u + 2) % RING)
                        if s > 0:
                            values(it, g, s - 1, u)
                        if s == 2:
                            turn_output(g, (u - 1) % RING, it + (1 if u else 0))
                        if s == 4 and not (last and u == RING - 1):
                            turn_maxima(g + 1, (u + 1) % 2)
                    values(it, g, NT - 1, u)

            with pe.Fori(0, G // RING - 1) as it:
                attend_pe(it, False)
            attend_pe(G // RING - 1, True)
            turn_output(G, RING - 1, G // RING, final=True)

            pe.wait_ge(b2_ready, 1)
            with pe.Fori(0, B) as b:
                pe.wait_ge(ao_ready, b + 1)
                pe.wait_ge(xn_ready, b)
                turn(ao, ao_turned)
                pe.wait_ge(ao_t_copied, b + 1)
                pe.wait_ge(res_seq, b)
                for m in range(NT):
                    last = mm(ps[:, 2, D * m:D * (m + 1)], ao_t[:, P * m:P * (m + 1)], proj_a[:, :],
                              start=True, stop=True)
                last.then_inc(proj_done, 1)
                pe.wait_ge(hn_ready, b * 2 + (B + 2))
                turn(hn, xn_turned)
                pe.wait_ge(xn_ready, b + 1)
                pe.wait_ge(gap_ready, b)
                for m in range(NT):
                    last = mm(ps[:, 3, E * m:E * (m + 1)], xn_b[:, P * m:P * (m + 1)], wr_a[:, :],
                              start=True, stop=True)
                last.then_inc(routed, 1)
                pe.wait_ge(w_split, b + 1)
                pe.wait_ge(w_t_copied, b)
                for m in range(NT):
                    last = nc.tensor.transpose(ps[:, 4, :].bitcast(bf16)[0:PARTS * E, P * m:P * (m + 1)],
                                               w_p[:, m, :, :].rearrange("p a e -> p (a e)"), ident_b[:, :])
                last.then_inc(w_turned, 1)
            pe.wait_ge(xn_kept, B)
            pe.wait_ge(w_t_copied, B)

            with pe.Fori(0, NCH // 2) as c2:
                for i in range(2):
                    n = c2 * 2 + i

                    def up(e2):
                        pe.wait_ge(hid_ready[e2 % 2], n * 2 + e2 // 2)
                        for k in range(2):
                            last = mm(ps[:, 2 * (e2 % 2) + k, :], w1_a[:, 2 * e2 + k, :], xn_all[:, ds(n * CH, CH)],
                                      start=True, stop=True)
                        last.then_inc(up_done, 1)

                    def spread(e):
                        pe.wait_ge(hid_scaled[(e - 2) % 4], n * 2 + (e + 2) // 4)
                        mm(ps[:, 4 + e % 2, :], pick[:, e, :], wt_all[:, ds(n * CH, CH)], start=True,
                           stop=True).then_inc(spread_done, 1)

                    def down(e):
                        if e == 0:
                            pe.wait_ge(ye_copied, n)
                        pe.wait_ge(hid_scaled[e % 4], n * 2 + (e // 4 + 1))
                        mm(ps[D * (e % 2):D * (e % 2 + 1), 6, :], w2_s[:, e, :], hid_w[:, e % 4, :],
                           start=(e < 2), stop=(e >= E - 2)).then_inc(down_done[e % 4], 1)

                    for e2 in range(E // 2):
                        up(e2)
                        for k in range(2):
                            spread(2 * e2 + k)
                        if e2:
                            for k in range(2):
                                down(2 * e2 - 2 + k)
                    for k in range(2):
                        down(E - 2 + k)
                    pe.wait_ge(out_ready, n)
                    pe.wait_ge(ye_copied, n + 1)
                    for t in range(CH // P):
                        y_out = ps[:, 7, D * t:D * (t + 1)]
                        for k in range(PARTS):
                            mm(y_out, wt_all[:, ds(n * CH + t * P, P)], b2_p[:, k, :], start=(k == 0), stop=False)
                        last = mm(y_out, ye_t[:, P * t:P * (t + 1)], pair_sum[:, :], start=False, stop=True)
                    last.then_inc(ffn_done, 1)


def kernel(**inputs):
    import concourse.bacc as bacc
    from concourse.bass_utils import run_bass_kernel_spmd

    a = {k: np.asarray(v) for k, v in inputs.items()}
    x = a["x"]
    tok = lambda n: a["L0_tok_" + n]
    att = lambda n: a["L0_attn_" + n]
    ffn = lambda n: a["L0_ffn_" + n]
    arrays = {
        "x_t": x.reshape(-1, x.shape[-1]).T,
        "gamma_t": tok("d_gamma_batched").T,
        "wq": tok("Wq"), "bq": tok("bq"), "wk": tok("Wk"), "bk": tok("bk"), "wv": tok("Wv"), "bv": tok("bv"),
        "wo": tok("Wo"), "bo": tok("bo"), "prelu_a": tok("prelu_a").reshape(1, 1),
        "qkv_w": att("qkv_w"), "qkv_b": att("qkv_b"), "proj_w": att("proj_w"), "proj_b": att("proj_b"),
        "rpb_rev": att("rpb_table").T[:, ::-1],
        "ffn_gamma": ffn("gamma"), "ffn_beta": ffn("beta"), "wr": ffn("Wr"), "br": ffn("br"),
        "w1": ffn("W1"), "b1": ffn("b1"), "w2": ffn("W2"), "b2": ffn("b2"),
    }
    nc = bacc.Bacc("TRN2", target_bir_lowering=False, num_devices=1)
    feeds, args = {}, []
    for name, v in arrays.items():
        v = np.ascontiguousarray(v)
        feeds[name] = v
        args.append(nc.dram_tensor(name, v.shape, mybir.dt.from_np(v.dtype), kind="ExternalInput").ap())
    out = nc.dram_tensor("out", (x.size // x.shape[-1], x.shape[-1]), mybir.dt.float32, kind="ExternalOutput").ap()
    vit_tower_kernel(nc, *args, out)
    r = run_bass_kernel_spmd(nc, [feeds], core_ids=[0])
    return r.results[0]["out"].reshape(x.shape[0], x.shape[2], x.shape[3])
```

```python
import numpy as np

import concourse.bass as bass
from concourse import mybir
from contextlib import ExitStack



def vit_tower_kernel(nc, x_t, gamma_t, tok_pack, aug_pack, wide_pack, b2_rows, rpb_rev, out):
    fp32 = mybir.dt.float32
    bf16 = mybir.dt.bfloat16
    ALU = mybir.AluOpType
    ACT = mybir.ActivationFunctionType
    AX = mybir.AxisListType.X

    P = 128
    D, N_ALL = x_t.shape
    T = gamma_t.shape[0]
    B = N_ALL // T
    NT = T // P
    HALF = T // 2
    NH, RPB = rpb_rev.shape
    DH = D // NH
    G = B * NH
    PARTS = 3
    E = b2_rows.shape[0] // PARTS
    HID = wide_pack.shape[0]
    MAXROW = 96
    RING = 4
    VC = 32
    FW = 2 * P
    CH = 512
    NCH = N_ALL // CH
    EPS = 1e-5
    SCALE = float(DH) ** -0.5
    LOWEST = -3.0e38
    ds = bass.ds

    qk_scratch = nc.dram_tensor("qk_parts", [PARTS, 2, G * DH, T], bf16).ap()
    v_scratch = nc.dram_tensor("v_padded", [G, P, NT * VC], fp32).ap()
    f_scratch = nc.dram_tensor("bias_parts", [G, PARTS, FW], bf16).ap()
    out_v = out.rearrange("(n p) d -> p n d", p=P)

    ctx = ExitStack()
    with ctx:
        def sb(name, shape, dt):
            return ctx.enter_context(nc.sbuf_tensor(name, shape, dt))

        def sem(name):
            return ctx.enter_context(nc.semaphore(name))

        gamma_sb = sb("gamma_sb", [P, NT, T], fp32)
        x_all = sb("x_all", [D + 1, N_ALL], fp32)
        tok_w = sb("tok_w", [D, tok_pack.shape[1]], fp32)
        A = D + 1
        wq_t, wk_t, wv_t = (tok_w[:, A * i:A * (i + 1)] for i in range(3))
        wo_s = tok_w[:, 3 * A:3 * A + D]
        gam_c = tok_w[:, 3 * A + D:3 * A + D + 1]
        bet_c = tok_w[:, 3 * A + D + 1:3 * A + D + 2]
        aug_w = sb("aug_w", [D + 1, aug_pack.shape[1]], fp32)
        qk_w = aug_w[:, 0:2 * D]
        vv_w = aug_w[:, 2 * D:3 * D]
        proj_a = aug_w[:, 3 * D:4 * D]
        wr_a = aug_w[:, 4 * D:4 * D + E]
        w1_a = aug_w[:, 4 * D + E:].rearrange("p (e h) -> p e h", e=E)
        wide_w = sb("wide_w", [P, wide_pack.shape[1]], fp32)
        w2_s = wide_w[:, 0:E * D].rearrange("p (e d) -> p e d", e=E)
        bo_b = wide_w[:, E * D:E * D + D]
        alpha = wide_w[:, E * D + D:E * D + D + 1]
        wqk = sb("wqk", [D + 1, D + 1], fp32)
        wvo = sb("wvo", [D + 1, D], fp32)
        b2_r = sb("b2_r", [PARTS * E, D], fp32)
        b2_rest = sb("b2_rest", [PARTS * E, D], fp32)
        b2_p = sb("b2_p", [P, PARTS, D], bf16)
        rpb_s = sb("rpb_s", [NH, RPB], fp32)
        f_diff = sb("f_diff", [NH, FW], fp32)
        f_rest = sb("f_rest", [NH, FW], fp32)
        f_p = sb("f_p", [NH, PARTS, FW], bf16)
        ident = sb("ident", [P, P], fp32)
        ident_b = sb("ident_b", [P, P], bf16)
        flip_b = sb("flip_b", [P, P], bf16)
        pair_sum = sb("pair_sum", [P, D], fp32)
        pick = sb("pick", [P, E, HID], bf16)
        rank = sb("rank", [P, B * NT, E], fp32)
        ones_done = sb("ones_done", [P, 1], fp32)
        mark = sb("mark", [P, 1], fp32)
        inv_d = sb("inv_d", [P, NT], fp32)
        eps_s = sb("eps_s", [P, NT], fp32)
        zeros = sb("zeros", [P, NT], fp32)
        half_pow = sb("half_pow", [P, NT], fp32)
        qk_scale = sb("qk_scale", [P, 1], fp32)

        g_t = sb("g_t", [D + 1, 2, T], fp32)
        vt_s = sb("vt_s", [P, HALF], fp32)
        v_s = sb("v_s", [P, 2, NT, D], fp32)
        gated = sb("gated", [P, 4, HALF], fp32)
        ret_t = sb("ret_t", [P, HALF], fp32)
        y_s = sb("y_s", [P, NT, D], fp32)
        neg_s = sb("neg_s", [P, NT, D], fp32)
        h_all = sb("h_all", [P, B * NT, D], fp32)

        xc = sb("xc", [P, 2, NT, D], fp32)
        sq = sb("sq", [P, NT, D], fp32)
        hn = sb("hn", [P, 2, NT, D], fp32)
        mean = sb("mean", [P, 2, NT], fp32)
        nmean = sb("nmean", [P, 2, NT], fp32)
        var = sb("var", [P, 2, NT], fp32)
        varm = sb("varm", [P, 2, NT], fp32)
        vare = sb("vare", [P, 2, NT], fp32)
        rstd = sb("rstd", [P, 2, NT], fp32)
        shrink = sb("shrink", [P, 2, 4, NT], fp32)
        vv_t = sb("vv_t", [P, HALF], fp32)
        hn_t = sb("hn_t", [D + 1, T], fp32)
        qk_h = sb("qk_h", [P, T], bf16)
        qk_rest = sb("qk_rest", [P, T], fp32)
        qk_m = sb("qk_m", [P, T], bf16)
        qk_l = sb("qk_l", [P, T], bf16)
        v_pad = sb("v_pad", [P, NH, NT, VC], fp32)

        q_ring = sb("q_ring", [P, RING, T], bf16)
        k_ring = sb("k_ring", [P, RING, T], bf16)
        x_ring = sb("x_ring", [P, RING, PARTS, P], bf16)
        v_ring = sb("v_ring", [P, RING, NT, VC], fp32)
        probs = sb("probs", [P, 4, T], fp32)
        nmax = sb("nmax", [P, 2, NT], fp32)
        max_rest = sb("max_rest", [P, 2, NT], fp32)
        max_p = sb("max_p", [P, 2, PARTS, NT], bf16)
        max_t = sb("max_t", [PARTS * NT, P], bf16)
        o_t = sb("o_t", [P, 2 * P], fp32)
        o_rec = sb("o_rec", [P, NT], fp32)
        attn = sb("attn", [P, NT, (G + 1) * DH], fp32)

        ao_t = sb("ao_t", [D + 1, 2, T], fp32)
        lg = sb("lg", [P, B * NT, E], fp32)
        lg2 = sb("lg2", [P, B * NT, E], fp32)
        eq = sb("eq", [P, B * NT, E], fp32)
        hot1 = sb("hot1", [P, B * NT, E], fp32)
        hot2 = sb("hot2", [P, B * NT, E], fp32)
        top1 = sb("top1", [P, B * NT], fp32)
        top2 = sb("top2", [P, B * NT], fp32)
        rk = sb("rk", [P, B * NT], fp32)
        gap = sb("gap", [P, B * NT], fp32)
        e_gap = sb("e_gap", [P, B * NT], fp32)
        den = sb("den", [P, B * NT], fp32)
        w_top1 = sb("w_top1", [P, B * NT], fp32)
        w_top2 = sb("w_top2", [P, B * NT], fp32)
        w_full = sb("w_full", [P, B * NT, E], fp32)
        w_rest = sb("w_rest", [P, B * NT, E], fp32)
        w_p = sb("w_p", [P, B * NT, PARTS, E], bf16)
        xn_all = gamma_sb[0:D + 1, 0:N_ALL // T, :].rearrange("p b t -> p (b t)")
        wt_all = gamma_sb[:, NT // 2:NT // 2 + N_ALL // (2 * T), :].rearrange("p b t -> p (b t)").bitcast(bf16)
        hid = probs[:, 0:2, :]
        hid_w = probs[:, 2:4, :].rearrange("p a (b n) -> p (a b) n", n=CH)
        ye_t = sb("ye_t", [P, CH], fp32)
        out_s = sb("out_s", [P, 2, CH // P, D], fp32)

        ps = ctx.enter_context(nc.psum_tensor("ps", [P, 8, 512], fp32))

        tok_w_loaded = sem("tok_w_loaded")
        wide_loaded = sem("wide_loaded")
        small_loaded = sem("small_loaded")
        aug_loaded = sem("aug_loaded")
        x_loaded = [sem(f"x_loaded{b}") for b in range(B)]
        gamma_loaded = [sem(f"gamma_loaded{i}") for i in range(NT // 2)]
        pool_seq = sem("pool_seq")
        dve_seq = sem("dve_seq")
        act_seq = sem("act_seq")
        consts_ready = sem("consts_ready")
        zeroed = sem("zeroed")
        pads_ready = sem("pads_ready")
        f_ready = sem("f_ready")
        b2_ready = sem("b2_ready")
        f_stored = sem("f_stored")
        folded = sem("folded")
        folded_copied = sem("folded_copied")
        g_projected = sem("g_projected")
        g_copied = sem("g_copied")
        vt_projected = sem("vt_projected")
        vt_copied = sem("vt_copied")
        v_turned = sem("v_turned")
        v_copied = sem("v_copied")
        tok_scored = sem("tok_scored")
        tok_gated = sem("tok_gated")
        tok_summed = sem("tok_summed")
        ret_copied = sem("ret_copied")
        y_turned = sem("y_turned")
        y_read = sem("y_read")
        h_ready = sem("h_ready")

        xc_ready = sem("xc_ready")
        sq_ready = sem("sq_ready")
        var_ready = sem("var_ready")
        vare_ready = sem("vare_ready")
        rstd_ready = sem("rstd_ready")
        hn_ready = sem("hn_ready")
        hn_turned = sem("hn_turned")
        hn_t_copied = sem("hn_t_copied")
        qk_done = sem("qk_done")
        vv_done = sem("vv_done")
        vv_copied = sem("vv_copied")
        vv_turned = sem("vv_turned")
        qk_h_ready = sem("qk_h_ready")
        qk_r_ready = sem("qk_r_ready")
        qk_m_ready = sem("qk_m_ready")
        qk_l_ready = sem("qk_l_ready")
        v_pad_ready = sem("v_pad_ready")
        qk_stored = [sem(f"qk_stored{i}") for i in range(PARTS)]
        v_stored = sem("v_stored")

        operands = [sem(f"operands{u}") for u in range(RING)]
        max_rows = [sem(f"max_rows{u}") for u in range(RING)]
        s1_ready = sem("s1_ready")
        s1_reduced = [sem(f"s1_reduced{i}") for i in range(2)]
        max_seq = sem("max_seq")
        max_split = sem("max_split")
        max_turned = [sem(f"max_turned{i}") for i in range(2)]
        max_copied = sem("max_copied")
        s2_ready = sem("s2_ready")
        exp_done = [sem(f"exp_done{i}") for i in range(2)]
        pv_done = [sem(f"pv_done{i}") for i in range(4)]
        o_copied = [sem(f"o_copied{u}") for u in range(RING)]
        o_turned = sem("o_turned")
        o_normed = sem("o_normed")

        wt_cleared = sem("wt_cleared")
        ao_turned = sem("ao_turned")
        ao_t_copied = sem("ao_t_copied")
        proj_done = sem("proj_done")
        xn_turned = sem("xn_turned")
        xn_ready = sem("xn_ready")
        routed = sem("routed")
        gap_ready = sem("gap_ready")
        e_gap_ready = sem("e_gap_ready")
        w_split = sem("w_split")
        w_turned = sem("w_turned")
        w_t_copied = sem("w_t_copied")

        up_done = sem("up_done")
        hid_ready = [sem(f"hid_ready{i}") for i in range(2)]
        spread_done = sem("spread_done")
        hid_scaled = [sem(f"hid_scaled{i}") for i in range(4)]
        down_done = [sem(f"down_done{i}") for i in range(4)]
        ye_copied = sem("ye_copied")
        ffn_done = sem("ffn_done")
        out_ready = sem("out_ready")
        route_seq = sem("route_seq")
        res_seq = sem("res_seq")
        rec_ready = sem("rec_ready")
        norm_seq = sem("norm_seq")
        y_seq = sem("y_seq")
        shrink_seq = sem("shrink_seq")
        out_stored = [sem(f"out_stored{i}") for i in range(2)]

        N_OPERANDS = 2 * PARTS + 2
        S1A, S2A, PVB, MISC = 0, 4, 6, 7
        max_ps = ps[:, MISC, :].bitcast(bf16)[0:PARTS * NT, 4 * P:5 * P]

        block = ctx.enter_context(nc.Block())

        @block.sync
        def _(sp):
            sp.dma_start(tok_w[:, :], tok_pack).then_inc(tok_w_loaded, 16)
            sp.dma_start(x_all[0:D, 0:T], x_t[:, 0:T]).then_inc(x_loaded[0], 16)
            gamma_v = gamma_t.rearrange("(s p) t -> p s t", p=P)
            sp.dma_start(gamma_sb[:, 0:2, :], gamma_v[:, 0:2, :]).then_inc(gamma_loaded[0], 16)
            sp.dma_start(wide_w[:, :], wide_pack).then_inc(wide_loaded, 16)
            sp.dma_start(gamma_sb[:, 2:4, :], gamma_v[:, 2:4, :]).then_inc(gamma_loaded[1], 16)
            sp.dma_start(x_all[0:D, T:2 * T], x_t[:, T:2 * T]).then_inc(x_loaded[1], 16)
            for i in range(2, NT // 2):
                sp.dma_start(gamma_sb[:, 2 * i:2 * i + 2, :], gamma_v[:, 2 * i:2 * i + 2, :]
                             ).then_inc(gamma_loaded[i], 16)
            sp.dma_start(aug_w[:, :], aug_pack).then_inc(aug_loaded, 16)
            sp.dma_start(rpb_s[:, :], rpb_rev).then_inc(small_loaded, 16)
            sp.dma_start(b2_r[:, :], b2_rows).then_inc(small_loaded, 16)
            for b in range(2, B):
                sp.dma_start(x_all[0:D, T * b:T * (b + 1)], x_t[:, T * b:T * (b + 1)]).then_inc(x_loaded[b], 16)
            for counter in (*exp_done, *pv_done, *o_copied, *max_turned, *out_stored):
                sp.sem_inc(counter, 1)

            sp.wait_ge(f_ready, 1)
            for b in range(B):
                sp.dma_start(f_scratch[NH * b:NH * b + NH, :, :], f_p[:, :, :]).then_inc(f_stored, 16)

            def load_head(g, u):
                rows = PARTS * DH
                for i in range(PARTS):
                    q_i = qk_scratch[i, 0, ds(g * DH, DH), :].rearrange("(o d) t -> o d t", o=1)
                    sp.dma_start(q_ring[rows * i:rows * (i + 1), u, :],
                                 q_i.to_broadcast([PARTS, DH, T])).then_inc(operands[u], 16)
                    sp.dma_start(k_ring[rows * i:rows * (i + 1), u, :],
                                 qk_scratch[:, 1, ds(g * DH, DH), :]).then_inc(operands[u], 16)
                f_g = f_scratch[ds(g, 1), :, :]
                sp.dma_start(x_ring[:, u, :, :],
                             bass.AP(tensor=f_g.tensor, offset=f_g.offset, ap=[[1, P], [FW, PARTS], [1, P]])
                             ).then_inc(operands[u], 16)
                sp.dma_start(v_ring[:, u, :, :],
                             v_scratch[ds(g, 1), :, :].rearrange("o p n -> (o p) n")).then_inc(operands[u], 16)

            for b in range(B):
                def store_parts(i, parts):
                    for qk in range(2):
                        sp.dma_start(qk_scratch[i, qk, D * b:D * b + D, :],
                                     parts[D * qk:D * qk + D, :]).then_inc(qk_stored[i], 16)

                sp.wait_ge(qk_h_ready, b + 1)
                store_parts(0, qk_h)
                sp.wait_ge(qk_m_ready, b + 1)
                store_parts(1, qk_m)
                sp.wait_ge(v_pad_ready, b + 1)
                sp.dma_start(v_scratch[NH * b:NH * b + NH, :, :].rearrange("h p n -> p h n"),
                             v_pad[:, :, :, :].rearrange("p h m c -> p h (m c)")).then_inc(v_stored, 16)
                sp.wait_ge(qk_l_ready, b + 1)
                store_parts(2, qk_l)
                if b in (0, B - 1):
                    for i in range(PARTS):
                        sp.wait_ge(qk_stored[i], 2 * 16 * (b + 1))
                    sp.wait_ge(v_stored, 16 * (b + 1))
                if b == 0:
                    sp.wait_ge(f_stored, 16 * B)
                    sp.wait_ge(pads_ready, 1)
                    for u in range(RING):
                        load_head(u, u)

            def send_max_rows(n, u):
                sp.wait_ge(max_copied, n + 1)
                sp.dma_start(q_ring[MAXROW:MAXROW + PARTS, u, :], max_t[:, :]).then_inc(max_rows[u], 16)

            send_max_rows(0, 0)
            with sp.Fori(0, G // RING - 1) as it:
                for u in range(RING):
                    send_max_rows(it * RING + (u + 1), (u + 1) % RING)
                    sp.wait_ge(o_copied[u], it + 2)
                    load_head(it * RING + (u + RING), u)
            for u in range(RING - 1):
                send_max_rows(G - RING + u + 1, u + 1)

            with sp.Fori(0, NCH // 2) as c2:
                for i in range(2):
                    sp.wait_ge(out_ready, c2 * 2 + (i + 1))
                    sp.dma_start(out_v[:, ds(c2 * (2 * CH // P) + i * (CH // P), CH // P), :],
                                 out_s[:, i, :, :]).then_inc(out_stored[i], 16)
            for i in range(2):
                sp.wait_ge(out_stored[i], 16 * (NCH // 2) + 1)

        @block.gpsimd
        def _(pool):
            seq = [0]

            def after(ins):
                seq[0] += 1
                ins.then_inc(pool_seq, 1)
                pool.wait_ge(pool_seq, seq[0])

            gp = nc.gpsimd
            for m in (ident[:, :], ident_b[:, :], flip_b[:, :], pair_sum[:, :], pick[:, :, :]):
                after(gp.memset(m, 0.0))

            def ones_where(m, base, pattern, mult):
                after(gp.affine_select(out=m, in_=m, compare_op=ALU.not_equal, fill=1.0, base=base,
                                       pattern=pattern, channel_multiplier=mult))

            ones_where(ident[:, :], 0, [[-1, P]], 1)
            ones_where(ident_b[:, :], 0, [[-1, P]], 1)
            ones_where(flip_b[:, :], 1 - P, [[1, P]], 1)
            for e in range(2):
                ones_where(pair_sum[:, :], -D * e, [[-1, D]], 1)
            for i in range(PARTS):
                ones_where(pick[:, :, :], -E * i, [[-1, E], [0, HID]], 1)
            gp.memset(ones_done[:, :], 0.0).then_inc(consts_ready, 1)

            pool.wait_ge(pads_ready, 1)

            def power(n):
                par = n % 2
                pool.wait_ge(var_ready, n + 1)
                gp.tensor_tensor(varm[:, par, :], var[:, par, :], inv_d[:, :], ALU.mult).then_inc(vare_ready, 1)
                pool.wait_ge(vare_ready, n * 2 + 1)
                gp.tensor_tensor(vare[:, par, :], varm[:, par, :], eps_s[:, :], ALU.add).then_inc(vare_ready, 1)
                pool.wait_ge(vare_ready, n * 2 + 2)
                return gp.tensor_tensor(rstd[:, par, :], vare[:, par, :], half_pow[:, :], ALU.pow)

            for b in range(B):
                power(b).then_inc(rstd_ready, 1)

            pool.wait_ge(h_ready, B)
            gp.memset(wt_all, 0.0).then_inc(wt_cleared, 1)
            pool.wait_ge(wt_cleared, 1)
            gp.memset(xn_all[D:D + 1, :], 1.0).then_inc(wt_cleared, 1)
            pool.wait_ge(wt_cleared, 2)

            with pool.Fori(0, G // 2) as g2:
                for v in range(2):
                    g = g2 * 2 + v
                    pool.wait_ge(s1_reduced[0], g * (NT // 2) + NT // 2)
                    pool.wait_ge(s1_reduced[1], g * (NT // 2) + NT // 2)
                    pool.wait_ge(max_turned[v], g2 + 1)
                    k = g * 3

                    def step(n, ins):
                        ins.then_inc(max_seq, 1)
                        pool.wait_ge(max_seq, k + n)

                    p0, p1, p2 = (max_p[:, v, i, :] for i in range(PARTS))
                    step(1, gp.tensor_tensor(p0, nmax[:, v, :], zeros[:, :], ALU.add))
                    step(2, gp.tensor_tensor(max_rest[:, v, :], nmax[:, v, :], p0, ALU.subtract))
                    step(3, gp.tensor_tensor(p1, max_rest[:, v, :], zeros[:, :], ALU.add))
                    gp.tensor_tensor(p2, max_rest[:, v, :], p1, ALU.subtract).then_inc(max_split, 1)

            for b in range(B):
                n, par = B + b, (B + b) % 2
                step = [5 * b]

                def then(ins):
                    step[0] += 1
                    ins.then_inc(shrink_seq, 1)
                    pool.wait_ge(shrink_seq, step[0])

                then(power(n))
                w = shrink[:, par]
                then(gp.tensor_tensor(w[:, 0, :], rstd[:, par, :], rstd[:, par, :], ALU.mult))
                then(gp.tensor_tensor(w[:, 1, :], w[:, 0, :], varm[:, par, :], ALU.mult))
                then(gp.tensor_tensor(w[:, 2, :], w[:, 1, :], eps_s[:, :], ALU.add))
                then(gp.tensor_tensor(w[:, 3, :], w[:, 2, :], half_pow[:, :], ALU.pow))
                gp.tensor_tensor(rstd[:, par, :], rstd[:, par, :], w[:, 3, :], ALU.mult).then_inc(rstd_ready, 1)

        @block.scalar
        def _(act):
            A = nc.scalar
            act.wait_ge(pads_ready, 1)

            def square(n):
                act.wait_ge(xc_ready, n + 1)
                act.wait_ge(var_ready, n)
                A.activation(sq[:, :, :], xc[:, n % 2, :, :], ACT.Square).then_inc(sq_ready, 1)

            def flat(a, b, rows=P):
                return ps[0:rows, a:b, :].rearrange("p a n -> p (a n)")

            def leave_g(b):
                act.wait_ge(g_projected, b + 1)
                if b >= 2:
                    act.wait_ge(tok_scored, (b - 1) * 2 * NT)
                A.activation(g_t[:, b % 2, :], flat(4, 6, D + 1), ACT.Copy).then_inc(g_copied, 1)
                act.wait_ge(vt_projected, b + 1)
                act.wait_ge(v_turned, b)
                A.activation(vt_s[:, :], ps[:, 6, :], ACT.Copy).then_inc(vt_copied, 1)

            def leave_v(b):
                act.wait_ge(v_turned, b + 1)
                if b >= 2:
                    act.wait_ge(tok_summed, (b - 1) * 2 * NT)
                A.activation(v_s[:, b % 2, :, :].rearrange("p (j c) d -> p c j d", j=2),
                             ps[:, 7, :].rearrange("p (c j d) -> p c j d", j=2, d=D),
                             ACT.Copy).then_inc(v_copied, 1)

            act.wait_ge(folded, 1)
            A.activation(wqk[:, :], ps[0:D + 1, 3, 0:D + 1], ACT.Copy).then_inc(folded_copied, 1)
            A.activation(wvo[:, :], ps[0:D + 1, 3, P:P + D], ACT.Copy).then_inc(folded_copied, 1)
            leave_g(0)
            leave_v(0)
            for b in range(B + 1):
                for u in range(2 * NT):
                    n = b - 1
                    if u == 0 and b > 0:
                        act.wait_ge(tok_summed, b * 2 * NT)
                        act.wait_ge(y_turned, n)
                        A.activation(ret_t[:, :], ps[:, 3, :], ACT.Copy).then_inc(ret_copied, 1)
                    if u == 4 and b + 1 < B:
                        leave_g(b + 1)
                    if u == 6 and b > 0:
                        square(n)
                    if u == 8 and b + 1 < B:
                        leave_v(b + 1)
                    if u == 10 and b > 0:
                        act.wait_ge(hn_turned, b)
                        act.wait_ge(vv_done, n)
                        A.activation(hn_t[0:D, :], flat(4, 6, D), ACT.Copy).then_inc(hn_t_copied, 1)
                    if u == 12 and b > 0:
                        act.wait_ge(qk_done, b)
                        act.wait_ge(qk_stored[0], n * 2 * 16)
                        A.activation(qk_h[:, :], flat(6, 8), ACT.Identity,
                                     scale=qk_scale[:, 0:1]).then_inc(qk_h_ready, 1)
                        act.wait_ge(vv_done, b)
                        A.activation(vv_t[:, :], ps[:, 4, :], ACT.Copy).then_inc(vv_copied, 1)
                    if u == 13 and b > 0:
                        act.wait_ge(qk_r_ready, b)
                        act.wait_ge(qk_stored[1], n * 2 * 16)
                        A.activation(qk_m[:, :], qk_rest[:, :], ACT.Copy).then_inc(qk_m_ready, 1)
                    if u == 14 and b > 0:
                        act.wait_ge(vv_turned, b)
                        act.wait_ge(v_stored, n * 16)
                        for j in range(2):
                            last = A.activation(
                                v_pad[:, :, NT // 2 * j:NT // 2 * (j + 1), 0:DH].rearrange("p h m c -> p m h c"),
                                ps[:, 5, :].rearrange("p (m j h c) -> p j m h c", j=2, h=NH, c=DH)[:, j], ACT.Copy)
                        last.then_inc(v_pad_ready, 1)

            def max_rows_copy(turned, par, sent, sent_slot):
                act.wait_ge(max_turned[par], turned + 1)
                if sent is not None:
                    act.wait_ge(max_rows[sent_slot], sent)
                A.activation(max_t[:, :], max_ps, ACT.Copy).then_inc(max_copied, 1)

            def attend_act(it, last):
                for u in range(RING):
                    g = it * RING + u
                    for s in range(NT):
                        for j in range(2):
                            act.wait_ge(s2_ready, g * (2 * NT) + (2 * s + j + 1))
                            if j == 0:
                                act.wait_ge(pv_done[s % 4], g * (NT // 4) + (s // 4 + 1))
                            A.activation(probs[:, s % 4, HALF * j:HALF * (j + 1)], ps[:, S2A + j, :],
                                         ACT.Exp).then_inc(exp_done[j], 1)
                        if s == 4 and not (last and u == RING - 1):
                            max_rows_copy(it * 2 + (u + 1) // 2 + 1, (u + 1) % 2, it * 16 + 16, u)
                    act.wait_ge(pv_done[3], g * (NT // 4) + (NT // 4 + 1))
                    act.wait_ge(o_turned, g + 1)
                    A.activation(o_t[:, :], ps[:, PVB, 0:2 * P], ACT.Copy).then_inc(o_copied[u], 1)

            max_rows_copy(1, 0, None, None)
            with act.Fori(0, G // RING - 1) as it:
                attend_act(it, False)
            attend_act(G // RING - 1, True)

            act.wait_ge(wt_cleared, 2)
            for t in range(B + 1):
                if t < B:
                    act.wait_ge(ao_turned, t + 1)
                    if t >= 2:
                        act.wait_ge(proj_done, t - 1)
                    A.activation(ao_t[0:D, t % 2, :], flat(2 * (t % 2), 2 * (t % 2) + 2, D),
                                 ACT.Copy).then_inc(ao_t_copied, 1)
                    square(B + t)
                if t > 0:
                    b = t - 1
                    act.wait_ge(xn_turned, t)
                    A.activation(xn_all[0:D, T * b:T * (b + 1)], flat(2 * (b % 2), 2 * (b % 2) + 2, D), ACT.Identity,
                                 scale=gam_c, bias=bet_c).then_inc(xn_ready, 1)
            act.wait_ge(gap_ready, 1)
            A.activation(e_gap[:, :], gap[:, :], ACT.Exp).then_inc(e_gap_ready, 1)
            for b in range(B):
                act.wait_ge(w_turned, b + 1)
                A.activation(wt_all[0:PARTS * E, T * b:T * (b + 1)], ps[:, b, :].bitcast(bf16)[0:PARTS * E, 0:T],
                             ACT.Copy).then_inc(w_t_copied, 1)

            def leave_ye(n):
                for k in (2, 3):
                    act.wait_ge(down_done[k], n * 2 + 2)
                act.wait_ge(ffn_done, n)
                A.activation(ye_t[:, :], ps[:, 6, :], ACT.Copy).then_inc(ye_copied, 1)

            def experts_act(c2, first):
                for i in range(2):
                    n = c2 * 2 + i
                    for e2 in range(E // 2):
                        act.wait_ge(up_done, n * (E // 2) + (e2 + 1))
                        if not (first and i == 0 and e2 < 2):
                            act.wait_ge(hid_scaled[(2 * e2 - 3) % 4], n * 2 + e2 // 2)
                        A.activation(hid[:, e2 % 2, :], flat(2 * (e2 % 2), 2 * (e2 % 2) + 2),
                                     ACT.Gelu).then_inc(hid_ready[e2 % 2], 1)
                        if e2 == 0 and not (first and i == 0):
                            leave_ye(n - 1)

            experts_act(0, True)
            with act.Fori(1, NCH // 2) as c2:
                experts_act(c2, False)
            leave_ye(NCH - 1)

        @block.vector
        def _(dve):
            V = nc.vector

            def chain(counter, base):
                count = [0]

                def step(ins):
                    count[0] += 1
                    ins.then_inc(counter, 1)
                    dve.wait_ge(counter, base + count[0])
                return step

            V.memset(v_pad[:, :, :, :], 0.0)
            V.memset(q_ring[D:P, :, :], 0.0)
            V.memset(k_ring[D:P, :, :], 0.0)
            V.memset(b2_p[:, :, :], 0.0)
            V.memset(f_diff[:, :], 0.0).then_inc(zeroed, 1)
            dve.wait_ge(zeroed, 1)
            V.memset(v_pad[:, :, :, DH:DH + 1], 1.0)
            V.memset(k_ring[MAXROW:MAXROW + PARTS, :, :], 1.0)
            for e in range(E):
                V.memset(rank[:, :, e:e + 1], float(E - e))
            for m, value in ((half_pow, -0.5), (inv_d, 1.0 / D), (eps_s, EPS), (zeros, 0.0), (o_t, 1.0)):
                V.memset(m[:, :], value)
            V.memset(qk_scale[0:D, :], SCALE)
            V.memset(qk_scale[D:P, :], 1.0)
            V.memset(x_all[D:D + 1, :], 1.0)
            V.memset(hn_t[D:D + 1, :], 1.0)
            V.memset(ao_t[D:D + 1, :, :], 1.0)
            V.memset(mark[:, :], 0.0).then_inc(pads_ready, 1)

            def small_tables():
                dve.wait_ge(small_loaded, 2 * 16)
                dve.wait_ge(pads_ready, 1)
                step = chain(dve_seq, 0)
                step(V.tensor_scalar(f_diff[:, P:P + RPB], rpb_s[:, :], rpb_s[:, 0:1], None, ALU.subtract))
                step(V.tensor_copy(f_p[:, 0, :], f_diff[:, :]))
                step(V.tensor_tensor(f_rest[:, :], f_diff[:, :], f_p[:, 0, :], ALU.subtract))
                step(V.tensor_copy(f_p[:, 1, :], f_rest[:, :]))
                V.tensor_tensor(f_p[:, 2, :], f_rest[:, :], f_p[:, 1, :], ALU.subtract).then_inc(f_ready, 1)
                rows = slice(0, PARTS * E)
                step(V.tensor_copy(b2_p[rows, 0, :], b2_r[:, :]))
                step(V.tensor_tensor(b2_rest[:, :], b2_r[:, :], b2_p[rows, 0, :], ALU.subtract))
                step(V.tensor_copy(b2_p[rows, 1, :], b2_rest[:, :]))
                V.tensor_tensor(b2_p[rows, 2, :], b2_rest[:, :], b2_p[rows, 1, :], ALU.subtract).then_inc(b2_ready, 1)

            def over_d(m):
                return m.rearrange("p (m o) -> p m o", o=1).to_broadcast([P, NT, D])

            def norm_center(src, n):
                par = n % 2
                step = chain(norm_seq, 2 * n)
                step(V.tensor_reduce(mean[:, par, :], src, AX, ALU.add))
                step(V.tensor_scalar(nmean[:, par, :], mean[:, par, :], -1.0 / D, None, ALU.mult))
                V.tensor_tensor(xc[:, par, :, :], src, over_d(nmean[:, par, :]), ALU.add).then_inc(xc_ready, 1)

            def norm_var(n):
                dve.wait_ge(sq_ready, n + 1)
                V.tensor_reduce(var[:, n % 2, :], sq[:, :, :], AX, ALU.add).then_inc(var_ready, 1)

            def norm_scale(n):
                dve.wait_ge(rstd_ready, n + 1)
                dve.wait_ge(xc_ready, n + 1)
                V.tensor_tensor(hn[:, n % 2, :, :], xc[:, n % 2, :, :], over_d(rstd[:, n % 2, :]),
                                ALU.mult).then_inc(hn_ready, 1)

            def row_max(g, s, par):
                dve.wait_ge(s1_ready, g * NT + (s + 1))
                bank = S1A + 2 * (s % 2)
                V.tensor_reduce(nmax[:, par, s:s + 1], ps[:, bank:bank + 2, :].rearrange("p a n -> p (a n)"),
                                AX, ALU.max, negate=True).then_inc(s1_reduced[s % 2], 1)

            for b in range(B + 1):
                n = b - 1
                for u in range(2 * NT):
                    if b < B:
                        s, j, at = u // 2, u % 2, b * 2 * NT + u
                        if b == 0:
                            dve.wait_ge(gamma_loaded[s // 2], 16)
                        dve.wait_ge(tok_scored, at + 1)
                        if at >= 4:
                            dve.wait_ge(tok_summed, at - 3)
                        V.tensor_tensor(gated[:, at % 4, :], ps[:, at % 3, :],
                                        gamma_sb[:, s, HALF * j:HALF * (j + 1)], ALU.mult).then_inc(tok_gated, 1)
                    if u == 12 and b == 0:
                        small_tables()
                    if b == B:
                        row_max(u // NT, u % NT, u // NT)
                    if b == 0:
                        continue
                    h_n = h_all[:, NT * n:NT * (n + 1), :]
                    if u == 3:
                        dve.wait_ge(y_turned, b)
                        if n == 0:
                            dve.wait_ge(wide_loaded, 16)
                        bo_m = bo_b.rearrange("p (a b d) -> p a b d", a=1, b=1).to_broadcast([P, NT // 2, 2, D])
                        V.tensor_tensor(y_s[:, :, :].rearrange("p (j c) d -> p c j d", j=2),
                                        ps[:, 7, :].rearrange("p (c j d) -> p c j d", j=2, d=D), bo_m,
                                        ALU.add).then_inc(y_read, 1)
                        dve.wait_ge(y_read, b)
                        V.tensor_scalar(neg_s[:, :, :], y_s[:, :, :], 0.0, alpha, ALU.min, ALU.mult).then_inc(y_seq, 1)
                    if u == 4:
                        dve.wait_ge(y_seq, b)
                        V.scalar_tensor_tensor(out=h_n, in0=y_s[:, :, :], scalar=0.0, in1=neg_s[:, :, :],
                                               op0=ALU.max, op1=ALU.add).then_inc(h_ready, 1)
                        dve.wait_ge(h_ready, b)
                        norm_center(h_n, n)
                    if u == 7:
                        norm_var(n)
                    if u == 9:
                        norm_scale(n)
                    if u == 12:
                        dve.wait_ge(qk_h_ready, b)
                        dve.wait_ge(qk_m_ready, n)
                        V.scalar_tensor_tensor(out=qk_rest[:, :], in0=ps[:, 6:8, :].rearrange("p a n -> p (a n)"),
                                               scalar=qk_scale[:, 0:1], in1=qk_h[:, :], op0=ALU.mult,
                                               op1=ALU.subtract).then_inc(qk_r_ready, 1)
                    if u == 14:
                        dve.wait_ge(qk_r_ready, b)
                        dve.wait_ge(qk_m_ready, b)
                        dve.wait_ge(qk_stored[2], n * 2 * 16)
                        V.tensor_tensor(qk_l[:, :], qk_rest[:, :], qk_m[:, :], ALU.subtract).then_inc(qk_l_ready, 1)

            def normalize(n):
                dve.wait_ge(o_turned, n + 1)
                o_v = ps[:, MISC, 0:2 * P].rearrange("p (c j x) -> p c j x", c=2, x=VC)
                rec_v = o_rec[:, :].rearrange("p (c j o) -> p c j o", c=2, o=1)
                V.reciprocal(rec_v, o_v[:, :, :, DH:DH + 1]).then_inc(rec_ready, 1)
                dve.wait_ge(rec_ready, n + 1)
                V.tensor_tensor(attn[:, :, ds(n * DH, DH)].rearrange("p (j c) d -> p c j d", c=2),
                                o_v[:, :, :, 0:DH], rec_v.to_broadcast([P, 2, NT // 2, DH]),
                                ALU.mult).then_inc(o_normed, 1)

            def attend_dve(it, last):
                for u in range(RING):
                    g = it * RING + u
                    for s in range(NT):
                        if not (last and u >= RING - 2):
                            if s == 0:
                                dve.wait_ge(max_split, g + 1)
                            row_max(g + 2, s, u % 2)
                        if s == 3:
                            normalize(g)

            with dve.Fori(0, G // RING - 1) as it:
                attend_dve(it, False)
            attend_dve(G // RING - 1, True)
            normalize(G)

            for t in range(B + 1):
                if t < B:
                    h_b = h_all[:, NT * t:NT * (t + 1), :]
                    dve.wait_ge(proj_done, t + 1)
                    V.tensor_tensor(h_b, h_b, ps[:, 4 + t % 2, :].rearrange("p (m d) -> p m d", d=D),
                                    ALU.add).then_inc(res_seq, 1)
                    dve.wait_ge(res_seq, t + 1)
                    norm_center(h_b, B + t)
                    norm_var(B + t)
                if t > 0:
                    norm_scale(B + t - 1)

            def over_e(m):
                return m[:, :].rearrange("p (m o) -> p m o", o=1).to_broadcast([P, B * NT, E])

            step = chain(route_seq, 0)
            dve.wait_ge(routed, B)
            step(V.tensor_copy(lg[:, :, :], ps[:, 6, 0:B * NT * E].rearrange("p (m e) -> p m e", e=E)))
            step(V.tensor_reduce(top1[:, :], lg[:, :, :], AX, ALU.max))
            step(V.tensor_tensor(eq[:, :, :], lg[:, :, :], over_e(top1), ALU.is_equal))
            step(V.tensor_tensor(eq[:, :, :], eq[:, :, :], rank[:, :, :], ALU.mult))
            step(V.tensor_reduce(rk[:, :], eq[:, :, :], AX, ALU.max))
            step(V.tensor_tensor(hot1[:, :, :], rank[:, :, :], over_e(rk), ALU.is_equal))
            step(V.scalar_tensor_tensor(out=lg2[:, :, :], in0=hot1[:, :, :], scalar=LOWEST, in1=lg[:, :, :],
                                        op0=ALU.mult, op1=ALU.add))
            step(V.tensor_reduce(top2[:, :], lg2[:, :, :], AX, ALU.max))
            V.tensor_tensor(gap[:, :], top2[:, :], top1[:, :], ALU.subtract).then_inc(gap_ready, 1)
            step(V.tensor_tensor(eq[:, :, :], lg2[:, :, :], over_e(top2), ALU.is_equal))
            step(V.tensor_tensor(eq[:, :, :], eq[:, :, :], rank[:, :, :], ALU.mult))
            step(V.tensor_reduce(rk[:, :], eq[:, :, :], AX, ALU.max))
            step(V.tensor_tensor(hot2[:, :, :], rank[:, :, :], over_e(rk), ALU.is_equal))
            dve.wait_ge(e_gap_ready, 1)
            step(V.tensor_scalar(den[:, :], e_gap[:, :], 1.0, None, ALU.add))
            step(V.reciprocal(w_top1[:, :], den[:, :]))
            step(V.tensor_tensor(w_top2[:, :], w_top1[:, :], e_gap[:, :], ALU.mult))
            step(V.tensor_tensor(hot1[:, :, :], hot1[:, :, :], over_e(w_top1), ALU.mult))
            step(V.tensor_tensor(hot2[:, :, :], hot2[:, :, :], over_e(w_top2), ALU.mult))
            step(V.tensor_tensor(w_full[:, :, :], hot1[:, :, :], hot2[:, :, :], ALU.add))
            step(V.tensor_copy(w_p[:, :, 0, :], w_full[:, :, :]))
            step(V.tensor_tensor(w_rest[:, :, :], w_full[:, :, :], w_p[:, :, 0, :], ALU.subtract))
            step(V.tensor_copy(w_p[:, :, 1, :], w_rest[:, :, :]))
            V.tensor_tensor(w_p[:, :, 2, :], w_rest[:, :, :], w_p[:, :, 1, :], ALU.subtract).then_inc(w_split, 1)

            def residual(n, i, stored):
                dve.wait_ge(ffn_done, n + 1)
                if stored is not None:
                    dve.wait_ge(out_stored[i], stored)
                V.tensor_tensor(out_s[:, i, :, :], ps[:, 7, 0:CH // P * D].rearrange("p (m d) -> p m d", d=D),
                                h_all[:, ds(n * (CH // P), CH // P), :], ALU.add).then_inc(out_ready, 1)

            def experts_dve(c2, first):
                for i in range(2):
                    n = c2 * 2 + i
                    for e in range(E):
                        dve.wait_ge(hid_ready[(e // 2) % 2], n * 2 + (e // 4 + 1))
                        dve.wait_ge(spread_done, n * E + (e + 1))
                        if not (first and i == 0 and e < 4):
                            dve.wait_ge(down_done[e % 4], n * 2 + e // 4)
                        V.tensor_tensor(hid_w[:, e % 4, :], hid[:, (e // 2) % 2, CH * (e % 2):CH * (e % 2 + 1)],
                                        ps[:, 4 + e % 2, :], ALU.mult).then_inc(hid_scaled[e % 4], 1)
                        if e == 3 and not (first and i == 0):
                            residual(n - 1, 1 - i, None if first else c2 * 16 + (1 if i else -15))

            experts_dve(0, True)
            with dve.Fori(1, NCH // 2) as c2:
                experts_dve(c2, False)
            residual(NCH - 1, 1, 16 * (NCH // 2 - 1) + 1)

        @block.tensor
        def _(pe):
            mm = nc.tensor.matmul

            def turn_four(dst_bank, src, done):
                for c in range(NT // 2):
                    last = nc.tensor.transpose(ps[:, dst_bank, P * c:P * (c + 1)], src[:, P * c:P * (c + 1)],
                                               ident[:, :])
                last.then_inc(done, 1)

            def turn(src, bank, done):
                for m in range(NT):
                    c = m % (NT // 2)
                    last = nc.tensor.transpose(ps[0:D, bank + m // (NT // 2), P * c:P * (c + 1)], src(m), ident[:, :])
                last.then_inc(done, 1)

            pe.wait_ge(tok_w_loaded, 16)
            mm(ps[0:D + 1, 3, 0:D + 1], wq_t, wk_t, start=True, stop=True)
            mm(ps[0:D + 1, 3, P:P + D], wv_t, wo_s, start=True, stop=True).then_inc(folded, 1)
            pe.wait_ge(consts_ready, 1)
            pe.wait_ge(pads_ready, 1)

            def project(b):
                pe.wait_ge(x_loaded[b], 16)
                if b >= 2:
                    pe.wait_ge(v_pad_ready, b - 2)
                    pe.wait_ge(qk_r_ready, b - 2)
                for j in range(2):
                    last = mm(ps[0:D + 1, 4 + j, :], wqk[:, :], x_all[:, T * b + HALF * j:T * b + HALF * (j + 1)],
                              start=True, stop=True)
                last.then_inc(g_projected, 1)
                for j in range(2):
                    last = mm(ps[D * j:D * (j + 1), 6, :], wvo[:, :], x_all[:, T * b + HALF * j:T * b + HALF * (j + 1)],
                              start=True, stop=True)
                last.then_inc(vt_projected, 1)

            def turn_v(b):
                pe.wait_ge(vt_copied, b + 1)
                if b >= 2:
                    pe.wait_ge(y_read, b - 1)
                turn_four(7, vt_s, v_turned)

            pe.wait_ge(folded_copied, 2)
            project(0)
            turn_v(0)

            def score(at):
                b, u = at // (2 * NT), at % (2 * NT)
                s, j = u // 2, u % 2
                if u == 0:
                    pe.wait_ge(g_copied, b + 1)
                if at >= 3:
                    pe.wait_ge(tok_gated, at - 2)
                mm(ps[:, at % 3, :], x_all[:, T * b + P * s:T * b + P * (s + 1)],
                   g_t[:, b % 2, HALF * j:HALF * (j + 1)], start=True, stop=True).then_inc(tok_scored, 1)

            def retain(at):
                b, u = at // (2 * NT), at % (2 * NT)
                s, j = u // 2, u % 2
                if u == 0:
                    pe.wait_ge(v_copied, b + 1)
                    pe.wait_ge(ret_copied, b)
                pe.wait_ge(tok_gated, at + 1)
                mm(ps[D * j:D * (j + 1), 3, :], v_s[:, b % 2, s, :], gated[:, at % 4, :], start=(s == 0),
                   stop=(s == NT - 1)).then_inc(tok_summed, 1)

            def scores_by_query(g, s, u):
                pe.wait_ge(s1_reduced[s % 2], g * (NT // 2) + s // 2)
                bank = S1A + 2 * (s % 2)
                for j in range(2):
                    last = mm(ps[:, bank + j, :], q_ring[0:MAXROW, u, P * s:P * (s + 1)],
                              k_ring[0:MAXROW, u, HALF * j:HALF * (j + 1)], start=True, stop=(s > 0 or j == 0))
                if s == 0:
                    for i in range(PARTS):
                        last = mm(ps[:, bank + 1, HALF - P:HALF], flip_b[:, :], x_ring[:, u, i, :],
                                  start=False, stop=(i == PARTS - 1))
                last.then_inc(s1_ready, 1)

            for at in range(2):
                score(at)
            for b in range(B + 1):
                n = b - 1
                for u in range(2 * NT):
                    at = b * 2 * NT + u
                    if at + 2 < B * 2 * NT:
                        score(at + 2)
                    if b < B:
                        retain(at)
                    if u == 2 and b > 0:
                        pe.wait_ge(ret_copied, b)
                        pe.wait_ge(qk_r_ready, n)
                        turn_four(7, ret_t, y_turned)
                    if u == 4 and b + 1 < B:
                        project(b + 1)
                    if u == 8 and b + 1 < B:
                        turn_v(b + 1)
                    if u == 10 and b > 0:
                        pe.wait_ge(hn_ready, b)
                        if b + 1 < B:
                            pe.wait_ge(g_copied, b + 2)
                        pe.wait_ge(v_pad_ready, n)
                        turn(lambda m: hn[:, n % 2, m, :], 4, hn_turned)
                    if u == 12 and b > 0:
                        if n == 0:
                            pe.wait_ge(aug_loaded, 16)
                        pe.wait_ge(hn_t_copied, b)
                        pe.wait_ge(y_read, b)
                        if b + 1 < B:
                            pe.wait_ge(vt_copied, b + 2)
                            pe.wait_ge(v_copied, b + 2)
                        for j in range(2):
                            last = mm(ps[:, 6 + j, :], qk_w, hn_t[:, HALF * j:HALF * (j + 1)], start=True, stop=True)
                        last.then_inc(qk_done, 1)
                        for j in range(2):
                            last = mm(ps[D * j:D * (j + 1), 4, :], vv_w, hn_t[:, HALF * j:HALF * (j + 1)],
                                      start=True, stop=True)
                        last.then_inc(vv_done, 1)
                    if u == 14 and b > 0:
                        pe.wait_ge(vv_copied, b)
                        turn_four(5, vv_t, vv_turned)
                    if b == B:
                        if u == 0:
                            pe.wait_ge(tok_gated, B * 2 * NT)
                        if u == 1:
                            pe.wait_ge(ret_copied, B)
                        if u % NT == 0:
                            pe.wait_ge(operands[u // NT], 16 * N_OPERANDS)
                        scores_by_query(u // NT, u % NT, u // NT)
            pe.wait_ge(qk_r_ready, B)
            pe.wait_ge(v_pad_ready, B)

            def scores_by_key(g, s, u):
                for j in range(2):
                    pe.wait_ge(exp_done[j], g * NT + (s + 1))
                    corner = s == NT - 1 and j == 0
                    last = mm(ps[:, S2A + j, :], k_ring[0:MAXROW + PARTS, u, P * s:P * (s + 1)],
                              q_ring[0:MAXROW + PARTS, u, HALF * j:HALF * (j + 1)], start=True, stop=not corner)
                    if corner:
                        for i in range(PARTS):
                            last = mm(ps[:, S2A, 0:P], x_ring[:, u, i, :], flip_b[:, :], start=False,
                                      stop=(i == PARTS - 1))
                    last.then_inc(s2_ready, 1)

            def values(it, g, m, u):
                if m == 0:
                    pe.wait_ge(o_copied[(u - 1) % RING], it + (2 if u else 1))
                for j in range(2):
                    pe.wait_ge(exp_done[j], g * NT + (m + 2))
                for j in range(4):
                    last = mm(ps[VC * j:VC * (j + 1), PVB, 0:2 * P], v_ring[:, u, m, :],
                              probs[:, m % 4, 2 * P * j:2 * P * (j + 1)], start=(m == 0), stop=(m == NT - 1))
                last.then_inc(pv_done[m % 4], 1)

            def turn_output(n, before, copied, final=False):
                pe.wait_ge(o_copied[before], copied)
                pe.wait_ge(max_copied, G if final else n + 1)
                if final:
                    pe.wait_ge(o_normed, G)
                for c in range(2):
                    last = nc.tensor.transpose(ps[:, MISC, P * c:P * (c + 1)], o_t[:, P * c:P * (c + 1)], ident[:, :])
                last.then_inc(o_turned, 1)

            def turn_maxima(g, par):
                pe.wait_ge(max_split, g + 1)
                pe.wait_ge(o_normed, g)
                nc.tensor.transpose(max_ps, max_p[:, par, :, :].rearrange("p a m -> p (a m)"),
                                    ident_b[:, :]).then_inc(max_turned[par], 1)

            turn_maxima(0, 0)

            def attend_pe(it, last):
                for u in range(RING):
                    g = it * RING + u
                    ahead = not (last and u >= RING - 2)
                    pe.wait_ge(max_rows[u], it * 16 + 16)
                    if ahead:
                        pe.wait_ge(operands[(u + 2) % RING],
                                   (it + (u + 2) // RING) * (16 * N_OPERANDS) + 16 * N_OPERANDS)
                    for s in range(NT):
                        scores_by_key(g, s, u)
                        if ahead:
                            scores_by_query(g + 2, s, (u + 2) % RING)
                        if s > 0:
                            values(it, g, s - 1, u)
                        if s == 2:
                            turn_output(g, (u - 1) % RING, it + (2 if u else 1))
                        if s == 4 and not (last and u == RING - 1):
                            turn_maxima(g + 1, (u + 1) % 2)
                    values(it, g, NT - 1, u)

            with pe.Fori(0, G // RING - 1) as it:
                attend_pe(it, False)
            attend_pe(G // RING - 1, True)
            turn_output(G, RING - 1, G // RING + 1, final=True)

            pe.wait_ge(b2_ready, 1)
            pe.wait_ge(o_normed, G + 1)
            for t in range(B + 1):
                if t < B:
                    if t >= 2:
                        pe.wait_ge(xn_ready, t - 1)
                    turn(lambda m: attn[:, m, D * t + DH:D * (t + 1) + DH], 2 * (t % 2), ao_turned)
                    pe.wait_ge(ao_t_copied, t + 1)
                    if t >= 2:
                        pe.wait_ge(res_seq, t - 1)
                    for m in range(NT):
                        last = mm(ps[:, 4 + t % 2, D * m:D * (m + 1)], ao_t[:, t % 2, P * m:P * (m + 1)], proj_a,
                                  start=True, stop=True)
                    last.then_inc(proj_done, 1)
                if t > 0:
                    b = t - 1
                    pe.wait_ge(hn_ready, B + t)
                    turn(lambda m: hn[:, (B + b) % 2, m, :], 2 * (b % 2), xn_turned)
                    pe.wait_ge(xn_ready, t)
                    for m in range(NT):
                        last = mm(ps[:, 6, E * (NT * b + m):E * (NT * b + m + 1)],
                                  xn_all[:, T * b + P * m:T * b + P * (m + 1)], wr_a, start=True, stop=True)
                    last.then_inc(routed, 1)
            pe.wait_ge(w_split, 1)
            for b in range(B):
                for m in range(NT):
                    last = nc.tensor.transpose(ps[:, b, :].bitcast(bf16)[0:PARTS * E, P * m:P * (m + 1)],
                                               w_p[:, NT * b + m, :, :].rearrange("p a e -> p (a e)"), ident_b[:, :])
                last.then_inc(w_turned, 1)
            pe.wait_ge(w_t_copied, B)

            def down(n, e):
                pe.wait_ge(hid_scaled[e % 4], n * 2 + (e // 4 + 1))
                mm(ps[D * (e % 2):D * (e % 2 + 1), 6, :], w2_s[:, e, :], hid_w[:, e % 4, :],
                   start=(e < 2), stop=(e >= E - 2)).then_inc(down_done[e % 4], 1)

            def finish(n, first):
                if not first:
                    pe.wait_ge(out_ready, n)
                pe.wait_ge(ye_copied, n + 1)
                for t in range(CH // P):
                    y_out = ps[:, 7, D * t:D * (t + 1)]
                    for k in range(PARTS):
                        mm(y_out, wt_all[:, ds(n * CH + t * P, P)], b2_p[:, k, :], start=(k == 0), stop=False)
                    last = mm(y_out, ye_t[:, P * t:P * (t + 1)], pair_sum[:, :], start=False, stop=True)
                last.then_inc(ffn_done, 1)

            def experts_pe(c2, first):
                for i in range(2):
                    n = c2 * 2 + i
                    start = first and i == 0
                    for e2 in range(E // 2):
                        if not (start and e2 < 2):
                            pe.wait_ge(hid_ready[e2 % 2], n * 2 + e2 // 2)
                        for k in range(2):
                            last = mm(ps[:, 2 * (e2 % 2) + k, :], w1_a[:, 2 * e2 + k, :], xn_all[:, ds(n * CH, CH)],
                                      start=True, stop=True)
                        last.then_inc(up_done, 1)
                        for e in (2 * e2, 2 * e2 + 1):
                            if not (start and e < 2):
                                pe.wait_ge(hid_scaled[(e - 2) % 4], n * 2 + (e + 2) // 4)
                            mm(ps[:, 4 + e % 2, :], pick[:, e, :], wt_all[:, ds(n * CH, CH)], start=True,
                               stop=True).then_inc(spread_done, 1)
                        for k in range(2):
                            if e2:
                                if e2 == 1 and k == 0 and not start:
                                    pe.wait_ge(ye_copied, n)
                                down(n, 2 * e2 - 2 + k)
                            elif not start:
                                down(n - 1, E - 2 + k)
                        if e2 == 1 and not start:
                            finish(n - 1, first and i == 1)

            experts_pe(0, True)
            with pe.Fori(1, NCH // 2) as c2:
                experts_pe(c2, False)
            for k in range(2):
                down(NCH - 1, E - 2 + k)
            finish(NCH - 1, False)


def kernel(**inputs):
    import concourse.bacc as bacc
    from concourse.bass_utils import run_bass_kernel_spmd

    a = {k: np.asarray(v) for k, v in inputs.items()}
    x = a["x"]
    tok = lambda n: a["L0_tok_" + n]
    att = lambda n: a["L0_attn_" + n]
    ffn = lambda n: a["L0_ffn_" + n]
    def aug(w, bias):
        return np.concatenate([w, bias.reshape(1, -1)], axis=0)

    w1 = ffn("W1")
    w2 = ffn("W2")
    arrays = {
        "x_t": x.reshape(-1, x.shape[-1]).T,
        "gamma_t": tok("d_gamma_batched").T,
        "tok_pack": np.concatenate([aug(tok("Wq"), tok("bq")).T, aug(tok("Wk"), tok("bk")).T,
                                    aug(tok("Wv"), tok("bv")).T, tok("Wo"), ffn("gamma").reshape(-1, 1),
                                    ffn("beta").reshape(-1, 1)], axis=1),
        "aug_pack": np.concatenate([aug(att("qkv_w"), att("qkv_b")), aug(att("proj_w"), att("proj_b")),
                                    aug(ffn("Wr"), ffn("br")),
                                    aug(w1.transpose(1, 0, 2).reshape(w1.shape[1], -1), ffn("b1"))], axis=1),
        "wide_pack": np.concatenate([w2.transpose(1, 0, 2).reshape(w2.shape[1], -1),
                                     np.broadcast_to(tok("bo"), (w2.shape[1], tok("bo").size)),
                                     np.broadcast_to(tok("prelu_a").reshape(1, 1), (w2.shape[1], 1))], axis=1),
        "b2_rows": np.concatenate([ffn("b2")] * 3, axis=0),
        "rpb_rev": att("rpb_table").T[:, ::-1],
    }
    nc = bacc.Bacc("TRN2", target_bir_lowering=False, num_devices=1)
    feeds, args = {}, []
    for name, v in arrays.items():
        v = np.ascontiguousarray(v)
        feeds[name] = v
        args.append(nc.dram_tensor(name, v.shape, mybir.dt.from_np(v.dtype), kind="ExternalInput").ap())
    out = nc.dram_tensor("out", (x.size // x.shape[-1], x.shape[-1]), mybir.dt.float32, kind="ExternalOutput").ap()
    vit_tower_kernel(nc, *args, out)
    r = run_bass_kernel_spmd(nc, [feeds], core_ids=[0])
    return r.results[0]["out"].reshape(x.shape[0], x.shape[2], x.shape[3])
```

```python
import numpy as np

import concourse.bass as bass
from concourse import mybir
from contextlib import ExitStack



def vit_tower_kernel(nc, x_t, gamma_t, tok_pack, aug_pack, up_pack, wide_pack, b2_rows, rpb_rev, out):
    fp32 = mybir.dt.float32
    bf16 = mybir.dt.bfloat16
    ALU = mybir.AluOpType
    ACT = mybir.ActivationFunctionType
    AX = mybir.AxisListType.X

    P = 128
    D, N_ALL = x_t.shape
    T = gamma_t.shape[0]
    B = N_ALL // T
    NT = T // P
    HALF = T // 2
    NH, RPB = rpb_rev.shape
    DH = D // NH
    G = B * NH
    PARTS = 3
    E = b2_rows.shape[0] // PARTS
    HID = wide_pack.shape[0]
    MAXROW = 96
    RING = 4
    VC = 32
    FW = 2 * P
    CH = 512
    NCH = N_ALL // CH
    WARM = (5, 2, 2)
    KX = 96
    EPS = 1e-5
    SCALE = float(DH) ** -0.5
    LOWEST = -3.0e38
    RT = N_ALL // P // 2
    ds = bass.ds

    qk_scratch = nc.dram_tensor("qk_parts", [G, 2, PARTS, DH, T], bf16).ap()
    v_scratch = nc.dram_tensor("v_padded", [G, P, NT * VC], fp32).ap()
    f_scratch = nc.dram_tensor("bias_parts", [G, PARTS, FW], bf16).ap()
    out_v = out.rearrange("(n p) d -> p n d", p=P)

    ctx = ExitStack()
    with ctx:
        def sb(name, shape, dt):
            return ctx.enter_context(nc.sbuf_tensor(name, shape, dt))

        def sem(name):
            return ctx.enter_context(nc.semaphore(name))

        gamma_sb = sb("gamma_sb", [P, NT, T], fp32)
        x_all = sb("x_all", [KX, N_ALL], fp32)
        tok_w = sb("tok_w", [D, tok_pack.shape[1]], fp32)
        A = D + 1
        wq_t, wk_t, wv_t = (tok_w[:, A * i:A * (i + 1)] for i in range(3))
        wo_s = tok_w[:, 3 * A:3 * A + D]
        aug_w = sb("aug_w", [D + 1, aug_pack.shape[1]], fp32)
        qk_w = aug_w[:, 0:2 * D]
        vv_w = aug_w[:, 2 * D:3 * D]
        UPS = E * HID
        up_w = sb("up_w", [P, UPS + VC], fp32)
        up_p = sb("up_p", [P, PARTS, UPS + VC], bf16)
        wide_w = sb("wide_w", [P, wide_pack.shape[1]], fp32)
        w2_s = wide_w[:, 0:E * D].rearrange("p (e d) -> p e d", e=E)
        bo_b = wide_w[:, E * D:E * D + D]
        alpha = wide_w[:, E * D + D:E * D + D + 1]
        proj_s = wide_w[:, E * D + D + 1:E * D + 2 * D + 1]
        proj_b, gam_c, bet_c = (wide_w[:, E * D + 2 * D + i:E * D + 2 * D + i + 1] for i in (1, 2, 3))
        br_b = wide_w[:, E * D + 2 * D + 4:E * D + 2 * D + 4 + E]
        b1_s = wide_w[:, E * D + 2 * D + 4 + E:E * D + 2 * D + 4 + 2 * E]
        proj2 = sb("proj2", [P, P], fp32)
        wqk = sb("wqk", [KX, KX], fp32)
        wvo = sb("wvo", [KX, D], fp32)
        b2_r = sb("b2_r", [PARTS * E, D], fp32)
        b2_rest = sb("b2_rest", [PARTS * E, D], fp32)
        b2_p = sb("b2_p", [P, PARTS, D], bf16)
        rpb_s = sb("rpb_s", [NH, RPB], fp32)
        f_diff = sb("f_diff", [NH, FW], fp32)
        f_rest = sb("f_rest", [NH, FW], fp32)
        f_p = sb("f_p", [NH, PARTS, FW], bf16)
        ident = sb("ident", [P, P], fp32)
        ident_b = sb("ident_b", [P, P], bf16)
        flip_b = sb("flip_b", [P, P], bf16)
        pick = sb("pick", [P, E, HID], bf16)
        rank = sb("rank", [P, B * NT, E], fp32)
        ones_done = sb("ones_done", [P, 1], fp32)
        inv_d = sb("inv_d", [P, NT], fp32)
        eps_s = sb("eps_s", [P, NT], fp32)
        inv_d2 = sb("inv_d2", [P, NT], fp32)
        eps2_s = sb("eps2_s", [P, NT], fp32)
        zeros = sb("zeros", [P, NT], fp32)
        half_pow = sb("half_pow", [P, NT], fp32)
        qk_scale = sb("qk_scale", [P, 1], fp32)

        g_t = sb("g_t", [KX, 2, T], fp32)
        vt_s = sb("vt_s", [P, HALF], fp32)
        v_s = sb("v_s", [P, 2, NT, D], fp32)
        gated = sb("gated", [P, 4, HALF], fp32)
        ret_t = sb("ret_t", [P, HALF], fp32)
        y_s = sb("y_s", [P, NT, D], fp32)
        neg_s = sb("neg_s", [P, NT, D], fp32)
        h_all = sb("h_all", [P, B * NT, D], fp32)

        xc = sb("xc", [P, 2, NT, D], fp32)
        sq = sb("sq", [P, NT, D], fp32)
        hn = sb("hn", [P, 2, NT, D], fp32)
        mean = sb("mean", [P, 2, NT], fp32)
        nmean = sb("nmean", [P, 2, NT], fp32)
        var = sb("var", [P, 2, NT], fp32)
        varm = sb("varm", [P, 2, NT], fp32)
        vare = sb("vare", [P, 2, NT], fp32)
        rstd = sb("rstd", [P, 2, NT], fp32)
        vv_t = sb("vv_t", [P, HALF], fp32)
        hn_t = sb("hn_t", [D + 1, T], fp32)
        qk_h = sb("qk_h", [P, T], bf16)
        qk_rest = sb("qk_rest", [P, T], fp32)
        qk_m = sb("qk_m", [P, T], bf16)
        qk_l = sb("qk_l", [P, T], bf16)
        v_pad = sb("v_pad", [P, NH, NT, VC], fp32)

        q_ring = sb("q_ring", [P, RING, T], bf16)
        k_ring = sb("k_ring", [P, RING, T], bf16)
        x_ring = sb("x_ring", [P, RING, PARTS, P], bf16)
        v_ring = sb("v_ring", [P, RING, NT, VC], fp32)
        probs = sb("probs", [P, 4, T], fp32)
        nmax = sb("nmax", [P, 2, NT], fp32)
        max_rest = sb("max_rest", [P, 2, NT], fp32)
        max_p = sb("max_p", [P, 2, PARTS, NT], bf16)
        max_t = sb("max_t", [PARTS * NT, P], bf16)
        o_t = sb("o_t", [P, 2 * P], fp32)
        o_rec = sb("o_rec", [P, NT], fp32)
        attn = sb("attn", [P, NT, G * DH], fp32)
        up_rest = attn[:, :, :].rearrange("p m d -> p (m d)")[:, 0:UPS + VC]

        ao_t = sb("ao_t", [P, HALF], fp32)
        pt_s = sb("pt_s", [P, HALF], fp32)
        x_parts = gated[:, 0:PARTS, :].rearrange("p a n -> p (a n)").bitcast(bf16).rearrange(
            "p (k i n) -> p k i n", k=2, i=PARTS)
        dve_rest = gated[:, PARTS, :]
        late = v_pad[:, :, :, :].rearrange("p h m c -> p (h m c)")
        xf = late[:, 0:2 * HALF].rearrange("p (k n) -> p k n", k=2)
        xf_rest = late[:, 2 * HALF:3 * HALF]
        lg_t = sb("lg_t", [P, HALF], fp32)
        lg = sb("lg", [P, B * NT, E], fp32)
        lg2 = sb("lg2", [P, B * NT, E], fp32)
        eq = sb("eq", [P, B * NT, E], fp32)
        hot1 = sb("hot1", [P, B * NT, E], fp32)
        hot2 = sb("hot2", [P, B * NT, E], fp32)
        top1 = sb("top1", [P, B * NT], fp32)
        top2 = sb("top2", [P, B * NT], fp32)
        rk = sb("rk", [P, B * NT], fp32)
        gap = sb("gap", [P, B * NT], fp32)
        e_gap = sb("e_gap", [P, B * NT], fp32)
        den = sb("den", [P, B * NT], fp32)
        w_top1 = sb("w_top1", [P, B * NT], fp32)
        w_top2 = sb("w_top2", [P, B * NT], fp32)
        w_full = sb("w_full", [P, B * NT, E], fp32)
        w_rest = sb("w_rest", [P, B * NT, E], fp32)
        w_p = sb("w_p", [P, 2, NT, 2, VC], bf16)
        x1_all = gamma_sb[:, 0:N_ALL // (2 * T), :].rearrange("p b t -> p (b t)").bitcast(bf16)
        x2_all = gamma_sb[:, NT // 4:NT // 4 + N_ALL // (2 * T), :].rearrange("p b t -> p (b t)").bitcast(bf16)
        wt_all = gamma_sb[:, NT // 2:NT // 2 + N_ALL // (2 * T), :].rearrange("p b t -> p (b t)").bitcast(bf16)
        hid = probs[:, 0:2, :]
        hid_w = probs[:, 2:4, :].rearrange("p a (b n) -> p (a b) n", n=CH)
        ye_t = late[:, 3 * HALF:3 * HALF + CH]
        out_half = y_s[:, 0:CH // P, :]
        out_s = neg_s[:, :, :].rearrange("p (k m) d -> p k m d", k=2)

        ps = ctx.enter_context(nc.psum_tensor("ps", [P, 8, 512], fp32))

        tok_w_loaded = sem("tok_w_loaded")
        wide_loaded = sem("wide_loaded")
        small_loaded = sem("small_loaded")
        aug_loaded = sem("aug_loaded")
        x_loaded = [sem(f"x_loaded{b}") for b in range(B)]
        gamma_loaded = [sem(f"gamma_loaded{i}") for i in range(NT // 2)]
        pool_seq = sem("pool_seq")
        dve_seq = sem("dve_seq")
        act_seq = sem("act_seq")
        consts_ready = sem("consts_ready")
        ident_ready = sem("ident_ready")
        warm_ready = sem("warm_ready")
        x_ones = sem("x_ones")
        w_cleared = sem("w_cleared")
        tables_ready = sem("tables_ready")
        pads_ready = sem("pads_ready")
        f_ready = sem("f_ready")
        b2_ready = sem("b2_ready")
        f_stored = sem("f_stored")
        folded = sem("folded")
        folded_copied = sem("folded_copied")
        g_projected = sem("g_projected")
        g_copied = sem("g_copied")
        vt_projected = sem("vt_projected")
        vt_copied = sem("vt_copied")
        v_turned = sem("v_turned")
        v_copied = sem("v_copied")
        tok_scored = sem("tok_scored")
        tok_gated = sem("tok_gated")
        tok_summed = sem("tok_summed")
        ret_copied = sem("ret_copied")
        y_turned = sem("y_turned")
        y_read = sem("y_read")
        h_ready = sem("h_ready")

        xc_ready = sem("xc_ready")
        sq_ready = sem("sq_ready")
        var_ready = sem("var_ready")
        vare_ready = sem("vare_ready")
        rstd_ready = sem("rstd_ready")
        hn_ready = sem("hn_ready")
        hn_turned = sem("hn_turned")
        hn_t_copied = sem("hn_t_copied")
        qk_done = sem("qk_done")
        vv_done = sem("vv_done")
        vv_copied = sem("vv_copied")
        vv_turned = sem("vv_turned")
        qk_h_ready = sem("qk_h_ready")
        qk_r_ready = sem("qk_r_ready")
        qk_m_ready = sem("qk_m_ready")
        qk_l_ready = sem("qk_l_ready")
        v_pad_ready = sem("v_pad_ready")
        qk_stored = [sem(f"qk_stored{i}") for i in range(PARTS)]
        v_stored = sem("v_stored")

        operands = [sem(f"operands{u}") for u in range(RING)]
        values_loaded = [sem(f"values_loaded{u}") for u in range(RING)]
        max_rows = [sem(f"max_rows{u}") for u in range(RING)]
        s1_ready = sem("s1_ready")
        s1_reduced = [sem(f"s1_reduced{i}") for i in range(2)]
        max_seq = sem("max_seq")
        max_split = sem("max_split")
        max_turned = [sem(f"max_turned{i}") for i in range(2)]
        max_copied = sem("max_copied")
        s2_ready = sem("s2_ready")
        exp_done = [sem(f"exp_done{i}") for i in range(2)]
        pv_done = [sem(f"pv_done{i}") for i in range(4)]
        o_copied = [sem(f"o_copied{u}") for u in range(RING)]
        o_turned = sem("o_turned")
        o_normed = sem("o_normed")

        wt_cleared = sem("wt_cleared")
        ao_turned = sem("ao_turned")
        ao_t_copied = sem("ao_t_copied")
        weights_padded = sem("weights_padded")
        up_loaded = sem("up_loaded")
        up_seq = sem("up_seq")
        up_split = sem("up_split")
        part_seq = sem("part_seq")
        x_rounded = sem("x_rounded")
        x_split = [sem(f"x_split{b}") for b in range(B)]
        x_placed = [sem(f"x_placed{b}") for b in range(B)]
        proj_done = sem("proj_done")
        pt_copied = sem("pt_copied")
        pt_turned = sem("pt_turned")
        xn_turned = sem("xn_turned")
        xf_ready = sem("xf_ready")
        routed = sem("routed")
        lg_t_copied = sem("lg_t_copied")
        lg_turned = sem("lg_turned")
        lg_read = sem("lg_read")
        gap_ready = sem("gap_ready")
        e_gap_ready = sem("e_gap_ready")
        w_split = sem("w_split")
        w_turned = sem("w_turned")
        w_t_copied = sem("w_t_copied")

        up_done = sem("up_done")
        hid_ready = [sem(f"hid_ready{i}") for i in range(2)]
        spread_done = sem("spread_done")
        hid_scaled = [sem(f"hid_scaled{i}") for i in range(4)]
        down_done = [sem(f"down_done{i}") for i in range(4)]
        ye_copied = sem("ye_copied")
        ffn_done = sem("ffn_done")
        half_added = sem("half_added")
        out_ready = sem("out_ready")
        route_seq = sem("route_seq")
        res_seq = sem("res_seq")
        rec_ready = sem("rec_ready")
        norm_seq = sem("norm_seq")
        y_seq = sem("y_seq")
        out_stored = [sem(f"out_stored{i}") for i in range(2)]

        N_OPERANDS = PARTS + 2
        S1A, S2A, PVB, MISC = 0, 4, 6, 7
        max_ps = ps[:, MISC, :].bitcast(bf16)[0:PARTS * NT, 4 * P:5 * P]
        FIRST_SCORES = {0: 1, 3: 2, 5: 1, 7: 1, 9: 1, 11: 1, 13: 2, 15: 7}
        FIRST_MAXIMA = {0: 1, 5: 1, 8: 2, 10: 4, 14: 1, 15: 7}

        block = ctx.enter_context(nc.Block())

        @block.sync
        def _(sp):
            sp.dma_start(tok_w[:, :], tok_pack).then_inc(tok_w_loaded, 16)
            sp.dma_start(x_all[0:D, 0:T], x_t[:, 0:T]).then_inc(x_loaded[0], 16)
            gamma_v = gamma_t.rearrange("(s p) t -> p s t", p=P)
            sp.dma_start(gamma_sb[:, 0:2, :], gamma_v[:, 0:2, :]).then_inc(gamma_loaded[0], 16)
            sp.dma_start(wide_w[:, :], wide_pack).then_inc(wide_loaded, 16)
            sp.dma_start(gamma_sb[:, 2:4, :], gamma_v[:, 2:4, :]).then_inc(gamma_loaded[1], 16)
            sp.dma_start(x_all[0:D, T:2 * T], x_t[:, T:2 * T]).then_inc(x_loaded[1], 16)
            for i in range(2, NT // 2):
                sp.dma_start(gamma_sb[:, 2 * i:2 * i + 2, :], gamma_v[:, 2 * i:2 * i + 2, :]
                             ).then_inc(gamma_loaded[i], 16)
            sp.dma_start(aug_w[:, :], aug_pack).then_inc(aug_loaded, 16)
            sp.dma_start(up_w[:, 0:UPS + E], up_pack).then_inc(up_loaded, 16)
            sp.dma_start(rpb_s[:, :], rpb_rev).then_inc(small_loaded, 16)
            sp.dma_start(b2_r[:, :], b2_rows).then_inc(small_loaded, 16)
            for b in range(2, B):
                sp.dma_start(x_all[0:D, T * b:T * (b + 1)], x_t[:, T * b:T * (b + 1)]).then_inc(x_loaded[b], 16)
            for counter in (*exp_done, *pv_done, *o_copied, *max_turned, *out_stored):
                sp.sem_inc(counter, 1)

            sp.wait_ge(f_ready, 1)
            for b in range(B):
                sp.dma_start(f_scratch[NH * b:NH * b + NH, :, :], f_p[:, :, :]).then_inc(f_stored, 16)

            def load_head(g, u):
                rows = PARTS * DH
                keys = qk_scratch[ds(g, 1), 1, :, :, :].rearrange("o i d t -> o (i d) t")
                sp.dma_start(k_ring[0:PARTS * rows, u, :],
                             keys.to_broadcast([PARTS, rows, T])).then_inc(operands[u], 16)
                for i in range(PARTS):
                    q_i = qk_scratch[ds(g, 1), 0, i, :, :]
                    sp.dma_start(q_ring[rows * i:rows * (i + 1), u, :],
                                 q_i.to_broadcast([PARTS, DH, T])).then_inc(operands[u], 16)
                f_g = f_scratch[ds(g, 1), :, :]
                sp.dma_start(x_ring[:, u, :, :],
                             bass.AP(tensor=f_g.tensor, offset=f_g.offset, ap=[[1, P], [FW, PARTS], [1, P]])
                             ).then_inc(operands[u], 16)
                sp.dma_start(v_ring[:, u, :, :],
                             v_scratch[ds(g, 1), :, :].rearrange("o p n -> (o p) n")).then_inc(values_loaded[u], 16)

            def send_max_rows(n, u):
                sp.wait_ge(max_copied, n + 1)
                sp.dma_start(q_ring[MAXROW:MAXROW + PARTS, u, :], max_t[:, :]).then_inc(max_rows[u], 16)

            for b in range(B):
                def store_parts(i, parts):
                    for qk in range(2):
                        sp.dma_start(qk_scratch[NH * b:NH * (b + 1), qk, i, :, :],
                                     parts[D * qk:D * qk + D, :]).then_inc(qk_stored[i], 16)

                sp.wait_ge(qk_h_ready, b + 1)
                store_parts(0, qk_h)
                sp.wait_ge(qk_m_ready, b + 1)
                store_parts(1, qk_m)
                if b == B - 1:
                    send_max_rows(0, 0)
                sp.wait_ge(v_pad_ready, b + 1)
                sp.dma_start(v_scratch[NH * b:NH * b + NH, :, :].rearrange("h p n -> p h n"),
                             v_pad[:, :, :, :].rearrange("p h m c -> p h (m c)")).then_inc(v_stored, 16)
                sp.wait_ge(qk_l_ready, b + 1)
                store_parts(2, qk_l)
                if b == 0:
                    for i in range(PARTS):
                        sp.wait_ge(qk_stored[i], 2 * 16)
                    sp.wait_ge(v_stored, 16)
                    sp.wait_ge(f_stored, 16 * B)
                    sp.wait_ge(pads_ready, 1)
                    for u in range(RING):
                        load_head(u, u)

            for i in range(PARTS):
                sp.wait_ge(qk_stored[i], 2 * 16 * B)
            sp.wait_ge(v_stored, 16 * B)

            def attend_sp(it, first, last):
                for u in range(RING):
                    if not (last and u == RING - 1):
                        send_max_rows(it * RING + (u + 1), (u + 1) % RING)
                    if not (first and u == 0) and not (last and u > 0):
                        sp.wait_ge(o_copied[(u - 1) % RING], it + (2 if u else 1))
                        load_head(it * RING + (u - 1 + RING), (u - 1) % RING)

            attend_sp(0, True, False)
            with sp.Fori(1, G // RING - 1) as it:
                attend_sp(it, False, False)
            attend_sp(G // RING - 1, False, True)

            for b in range(B):
                sp.wait_ge(x_split[b], 1)
                for j in range(2):
                    cols = slice(T * b + HALF * j, T * b + HALF * (j + 1))
                    for to, half, i in ((x1_all, 0, 0), (x1_all, 1, 1), (x2_all, 0, 2), (x2_all, 1, 0)):
                        sp.dma_start(to[D * half:D * (half + 1), cols],
                                     x_parts[D * j:D * (j + 1), b % 2, i, :]).then_inc(x_placed[b], 16)

            with sp.Fori(0, NCH // 2) as c2:
                for i in range(2):
                    sp.wait_ge(out_ready, c2 * 2 + (i + 1))
                    sp.dma_start(out_v[:, ds(c2 * (2 * CH // P) + i * (CH // P), CH // P), :],
                                 out_s[:, i, :, :]).then_inc(out_stored[i], 16)
            for i in range(2):
                sp.wait_ge(out_stored[i], 16 * (NCH // 2) + 1)

        @block.gpsimd
        def _(pool):
            seq = [0]

            def after(ins):
                seq[0] += 1
                ins.then_inc(pool_seq, 1)
                pool.wait_ge(pool_seq, seq[0])

            gp = nc.gpsimd
            def ones_where(m, base, pattern, mult):
                return gp.affine_select(out=m, in_=m, compare_op=ALU.not_equal, fill=1.0, base=base,
                                        pattern=pattern, channel_multiplier=mult)

            after(gp.memset(ident[:, :], 0.0))
            ones_where(ident[:, :], 0, [[-1, P]], 1).then_inc(ident_ready, 1)
            for m, value in ((f_diff[:, :], 0.0), (b2_p[:, :, :], 0.0), (q_ring[D:P, :, :], 0.0),
                             (k_ring[D:P, :, :], 0.0), (k_ring[MAXROW:MAXROW + PARTS, :, :], 1.0)):
                after(gp.memset(m, value))
            after(gp.memset(v_pad[:, :, :, :], 0.0))
            after(gp.memset(v_pad[:, :, :, DH:DH + 1], 1.0))
            for m, value in ((hn_t[D:D + 1, :], 1.0), (proj2[:, :], 0.0), (up_w[:, UPS + E:], 0.0),
                             (w_p[:, :, :, :, :], 0.0)):
                after(gp.memset(m, value))
            gp.memset(flip_b[:, :], 0.0).then_inc(pads_ready, 1)
            pool.wait_ge(pads_ready, 1)
            for m in (ident_b[:, :], pick[:, :, :]):
                after(gp.memset(m, 0.0))
            after(ones_where(ident_b[:, :], 0, [[-1, P]], 1))
            after(ones_where(flip_b[:, :], 1 - P, [[1, P]], 1))
            for i in range(PARTS):
                after(ones_where(pick[:, :, :], -E * i, [[-1, E], [0, HID]], 1))
            gp.memset(ones_done[:, :], 0.0).then_inc(consts_ready, 1)
            pool.wait_ge(up_loaded, 16)
            after(gp.tensor_copy(up_p[:, 0, :], up_w[:, :]))
            after(gp.tensor_tensor(up_rest, up_w[:, :], up_p[:, 0, :], ALU.subtract))
            after(gp.tensor_copy(up_p[:, 1, :], up_rest))
            after(gp.tensor_copy(up_p[0:D, 2, :], up_p[0:D, 0, :]))
            gp.tensor_tensor(up_p[D:P, 2, :], up_rest[D:P, :], up_p[D:P, 1, :], ALU.subtract).then_inc(up_split, 1)
            pool.wait_ge(up_split, 1)
            pool.wait_ge(tables_ready, 1)

            def power(n):
                par = n % 2
                over, add = (inv_d, eps_s) if n < B else (inv_d2, eps2_s)
                pool.wait_ge(var_ready, n + 1)
                gp.tensor_tensor(varm[:, par, :], var[:, par, :], over[:, :], ALU.mult).then_inc(vare_ready, 1)
                pool.wait_ge(vare_ready, n * 2 + 1)
                gp.tensor_tensor(vare[:, par, :], varm[:, par, :], add[:, :], ALU.add).then_inc(vare_ready, 1)
                pool.wait_ge(vare_ready, n * 2 + 2)
                return gp.tensor_tensor(rstd[:, par, :], vare[:, par, :], half_pow[:, :], ALU.pow)

            for b in range(B):
                power(b).then_inc(rstd_ready, 1)

            def split_maxima(g2):
                for v in range(2):
                    g = g2 * 2 + v
                    pool.wait_ge(s1_reduced[0], g * (NT // 2) + NT // 2)
                    pool.wait_ge(s1_reduced[1], g * (NT // 2) + NT // 2)
                    pool.wait_ge(max_turned[v], g2 + 1)
                    k = g * 3

                    def step(n, ins):
                        ins.then_inc(max_seq, 1)
                        pool.wait_ge(max_seq, k + n)

                    p0, p1, p2 = (max_p[:, v, i, :] for i in range(PARTS))
                    step(1, gp.tensor_tensor(p0, nmax[:, v, :], zeros[:, :], ALU.add))
                    step(2, gp.tensor_tensor(max_rest[:, v, :], nmax[:, v, :], p0, ALU.subtract))
                    step(3, gp.tensor_tensor(p1, max_rest[:, v, :], zeros[:, :], ALU.add))
                    gp.tensor_tensor(p2, max_rest[:, v, :], p1, ALU.subtract).then_inc(max_split, 1)

            split_maxima(0)
            pool.wait_ge(h_ready, B)
            gp.memset(wt_all, 0.0).then_inc(wt_cleared, 1)
            pool.wait_ge(wt_cleared, 1)
            with pool.Fori(1, G // 2) as g2:
                split_maxima(g2)

            for b in range(B):
                power(B + b).then_inc(rstd_ready, 1)
            b = B - 2
            x0, x1, x2 = (x_parts[:, b % 2, i, :] for i in range(PARTS))
            pool.wait_ge(xf_ready, b + 1)
            after(gp.tensor_tensor(xf_rest, xf[:, b % 2, :], x0, ALU.subtract))
            after(gp.tensor_tensor(x1, xf_rest, zeros[:, 0:1].to_broadcast([P, HALF]), ALU.add))
            gp.tensor_tensor(x2, xf_rest, x1, ALU.subtract).then_inc(x_split[b], 1)

        @block.scalar
        def _(act):
            A = nc.scalar

            def square(n):
                act.wait_ge(xc_ready, n + 1)
                act.wait_ge(var_ready, n)
                A.activation(sq[:, :, :], xc[:, n % 2, :, :], ACT.Square).then_inc(sq_ready, 1)

            def flat(a, b, rows=P):
                return ps[0:rows, a:b, :].rearrange("p a n -> p (a n)")

            def leave_g(b):
                act.wait_ge(g_projected, b + 1)
                if b >= 2:
                    act.wait_ge(tok_scored, (b - 1) * 2 * NT)
                A.activation(g_t[:, b % 2, :], flat(4, 6, KX), ACT.Copy).then_inc(g_copied, 1)
                act.wait_ge(vt_projected, b + 1)
                act.wait_ge(v_turned, b)
                A.activation(vt_s[:, :], ps[:, 6, :], ACT.Copy).then_inc(vt_copied, 1)

            def leave_v(b):
                act.wait_ge(v_turned, b + 1)
                if b >= 2:
                    act.wait_ge(tok_summed, (b - 1) * 2 * NT)
                A.activation(v_s[:, b % 2, :, :].rearrange("p (j c) d -> p c j d", j=2),
                             ps[:, 7, :].rearrange("p (c j d) -> p c j d", j=2, d=D),
                             ACT.Copy).then_inc(v_copied, 1)

            act.wait_ge(folded, 1)
            act.wait_ge(w_cleared, 1)
            A.activation(wqk[0:D + 1, 0:D + 1], ps[0:D + 1, 3, 0:D + 1], ACT.Copy).then_inc(folded_copied, 1)
            A.activation(wvo[0:D + 1, :], ps[0:D + 1, 3, P:P + D], ACT.Copy).then_inc(folded_copied, 1)
            leave_g(0)
            leave_v(0)
            def max_rows_copy(turned, par, sent, sent_slot):
                act.wait_ge(max_turned[par], turned + 1)
                if sent is not None:
                    act.wait_ge(max_rows[sent_slot], sent)
                A.activation(max_t[:, :], max_ps, ACT.Copy).then_inc(max_copied, 1)

            for b in range(B + 1):
                for u in range(2 * NT):
                    n = b - 1
                    if u == 0 and b > 0:
                        act.wait_ge(tok_summed, b * 2 * NT)
                        act.wait_ge(y_turned, n)
                        A.activation(ret_t[:, :], ps[:, 3, :], ACT.Copy).then_inc(ret_copied, 1)
                    if u == 4 and b + 1 < B:
                        leave_g(b + 1)
                    if u == 6 and b > 0:
                        square(n)
                    if u == 8 and b + 1 < B:
                        leave_v(b + 1)
                    if u == 10 and b > 0:
                        act.wait_ge(hn_turned, b)
                        act.wait_ge(pads_ready, 1)
                        act.wait_ge(vv_done, n)
                        A.activation(hn_t[0:D, :], flat(4, 6, D), ACT.Copy).then_inc(hn_t_copied, 1)
                    if u == 12 and b > 0:
                        act.wait_ge(qk_done, b)
                        act.wait_ge(tables_ready, 1)
                        act.wait_ge(qk_stored[0], n * 2 * 16)
                        A.activation(qk_h[:, :], flat(6, 8), ACT.Identity,
                                     scale=qk_scale[:, 0:1]).then_inc(qk_h_ready, 1)
                        act.wait_ge(vv_done, b)
                        A.activation(vv_t[:, :], ps[:, 4, :], ACT.Copy).then_inc(vv_copied, 1)
                    if u == 13 and b > 0:
                        act.wait_ge(qk_r_ready, b)
                        act.wait_ge(qk_stored[1], n * 2 * 16)
                        A.activation(qk_m[:, :], qk_rest[:, :], ACT.Copy).then_inc(qk_m_ready, 1)
                        if b == B:
                            max_rows_copy(1, 0, None, None)
                    if u == 14 and b > 0:
                        act.wait_ge(vv_turned, b)
                        act.wait_ge(v_stored, n * 16)
                        for j in range(2):
                            last = A.activation(
                                v_pad[:, :, NT // 2 * j:NT // 2 * (j + 1), 0:DH].rearrange("p h m c -> p m h c"),
                                ps[:, 5, :].rearrange("p (m j h c) -> p j m h c", j=2, h=NH, c=DH)[:, j], ACT.Copy)
                        last.then_inc(v_pad_ready, 1)

            def output_copy(g, u):
                act.wait_ge(pv_done[3], g * (NT // 4) + 1)
                act.wait_ge(o_turned, g - 1)
                A.activation(o_t[:, :], ps[:, PVB, 0:2 * P], ACT.Copy).then_inc(o_copied[(u - 1) % RING], 1)

            def attend_act(it, first, last):
                for u in range(RING):
                    g = it * RING + u
                    for s in range(NT):
                        for j in range(2):
                            act.wait_ge(s2_ready, g * (2 * NT) + (2 * s + j + 1))
                            if j == 0:
                                act.wait_ge(pv_done[s % 4], g * (NT // 4) + (s // 4 + 1))
                            A.activation(probs[:, s % 4, HALF * j:HALF * (j + 1)], ps[:, S2A + j, :],
                                         ACT.Exp).then_inc(exp_done[j], 1)
                        if s == 1 and not (first and u == 0):
                            output_copy(g, u)
                        if s == 2 and not (last and u == RING - 1):
                            max_rows_copy(it * 2 + (u + 1) // 2 + 1, (u + 1) % 2, it * 16 + 16, u)

            attend_act(0, True, False)
            with act.Fori(1, G // RING - 1) as it:
                attend_act(it, False, False)
            attend_act(G // RING - 1, False, True)
            output_copy(G, 0)

            def logits_copy(h):
                act.wait_ge(routed, 2 * h + 2)
                act.wait_ge(lg_turned, h)
                A.activation(lg_t[:, :], ps[:, 7 if h else 4, :], ACT.Copy).then_inc(lg_t_copied, 1)

            def xn_copy(b):
                src = ps[:, 7, :]
                act.wait_ge(xn_turned, b + 1)
                act.wait_ge(x_split[b - 2], 1)
                act.wait_ge(x_placed[b - 2], 8 * 16)
                A.activation(xf[:, b % 2, :], src, ACT.Identity, scale=gam_c, bias=bet_c)
                A.activation(x_parts[:, b % 2, 0, :], src, ACT.Identity, scale=gam_c, bias=bet_c
                             ).then_inc(xf_ready, 1)

            def exp_gap(h):
                act.wait_ge(gap_ready, h + 1)
                A.activation(e_gap[:, RT * h:RT * (h + 1)], gap[:, RT * h:RT * (h + 1)], ACT.Exp
                             ).then_inc(e_gap_ready, 1)

            def weights_copy(b):
                h, k = b // 2, b % 2
                act.wait_ge(w_turned, h + 1)
                A.activation(wt_all[0:PARTS * E, T * b:T * (b + 1)],
                             ps[:, 7 if h else 6, :].bitcast(bf16)[VC * k:VC * k + PARTS * E, 0:T],
                             ACT.Copy).then_inc(w_t_copied, 1)

            act.wait_ge(wt_cleared, 1)
            act.wait_ge(ao_turned, B)
            A.activation(ao_t[:, :], ps[:, 0, :], ACT.Copy).then_inc(ao_t_copied, 1)
            act.wait_ge(proj_done, B)
            A.activation(pt_s[:, :], ps[:, 2, :], ACT.Identity, bias=proj_b).then_inc(pt_copied, 1)
            logits_copy(0)
            exp_gap(0)

            def leave_ye(n):
                for k in (2, 3):
                    act.wait_ge(down_done[k], n * 2 + 2)
                act.wait_ge(ffn_done, n)
                A.activation(ye_t, ps[:, 6, :], ACT.Copy).then_inc(ye_copied, 1)

            WITHIN = {(0, 1): [(weights_copy, 0), (weights_copy, 1), (xn_copy, 2)], (0, 3): [(xn_copy, 3)],
                      (1, 3): [(logits_copy, 1)], (2, 2): [(exp_gap, 1)],
                      (3, 0): [(weights_copy, 2), (weights_copy, 3)]}

            def experts_act(c2, first, peeled):
                for i in range(2):
                    n = c2 * 2 + i
                    for e2 in range(E // 2):
                        act.wait_ge(up_done, n * (E // 2) + (e2 + 1))
                        if not (first and i == 0 and e2 < 2):
                            act.wait_ge(hid_scaled[(2 * e2 - 3) % 4], n * 2 + e2 // 2)
                        for k in range(2):
                            last = A.activation(hid[:, e2 % 2, CH * k:CH * (k + 1)], ps[:, 2 * (e2 % 2) + k, :],
                                                ACT.Gelu, bias=b1_s[:, 2 * e2 + k:2 * e2 + k + 1])
                        last.then_inc(hid_ready[e2 % 2], 1)
                        if e2 == 0 and not (first and i == 0):
                            leave_ye(n - 1)
                        for stage, arg in WITHIN.get((n, e2), []) if peeled else []:
                            stage(arg)

            experts_act(0, True, True)
            experts_act(1, False, True)
            with act.Fori(2, NCH // 2) as c2:
                experts_act(c2, False, False)
            leave_ye(NCH - 1)

        @block.vector
        def _(dve):
            V = nc.vector

            def chain(counter, base):
                count = [0]

                def step(ins):
                    count[0] += 1
                    ins.then_inc(counter, 1)
                    dve.wait_ge(counter, base + count[0])
                return step

            V.memset(sq[:, :, :], 0.0).then_inc(warm_ready, 1)
            V.memset(wqk[:, :], 0.0)
            V.memset(wvo[:, :], 0.0).then_inc(w_cleared, 1)
            V.memset(x_all[D:KX, 0:T], 1.0).then_inc(x_ones, 1)
            for m, value in ((half_pow, -0.5), (inv_d, 1.0 / D), (eps_s, EPS), (inv_d2, (1.0 + EPS) / D),
                             (eps2_s, EPS * EPS), (zeros, 0.0)):
                V.memset(m[:, :], value)
            V.memset(qk_scale[0:D, :], SCALE)
            V.memset(qk_scale[D:P, :], 1.0).then_inc(tables_ready, 1)
            for b in range(1, B):
                V.memset(x_all[D:KX, T * b:T * (b + 1)], 1.0).then_inc(x_ones, 1)
            for e in range(E):
                V.memset(rank[:, :, e:e + 1], float(E - e))

            def small_tables():
                dve.wait_ge(small_loaded, 2 * 16)
                dve.wait_ge(pads_ready, 1)
                step = chain(dve_seq, 0)
                step(V.tensor_scalar(f_diff[:, P:P + RPB], rpb_s[:, :], rpb_s[:, 0:1], None, ALU.subtract))
                step(V.tensor_copy(f_p[:, 0, :], f_diff[:, :]))
                step(V.tensor_tensor(f_rest[:, :], f_diff[:, :], f_p[:, 0, :], ALU.subtract))
                step(V.tensor_copy(f_p[:, 1, :], f_rest[:, :]))
                V.tensor_tensor(f_p[:, 2, :], f_rest[:, :], f_p[:, 1, :], ALU.subtract).then_inc(f_ready, 1)
                rows = slice(0, PARTS * E)
                step(V.tensor_copy(b2_p[rows, 0, :], b2_r[:, :]))
                step(V.tensor_tensor(b2_rest[:, :], b2_r[:, :], b2_p[rows, 0, :], ALU.subtract))
                step(V.tensor_copy(b2_p[rows, 1, :], b2_rest[:, :]))
                V.tensor_tensor(b2_p[rows, 2, :], b2_rest[:, :], b2_p[rows, 1, :], ALU.subtract).then_inc(b2_ready, 1)
                dve.wait_ge(wide_loaded, 16)
                for j in range(2):
                    last = V.tensor_copy(proj2[D * j:D * (j + 1), D * j:D * (j + 1)], proj_s[D * j:D * (j + 1), :])
                last.then_inc(weights_padded, 1)

            def over_d(m):
                return m.rearrange("p (m o) -> p m o", o=1).to_broadcast([P, NT, D])

            def norm_center(src, n):
                par = n % 2
                step = chain(norm_seq, 2 * n)
                step(V.tensor_reduce(mean[:, par, :], src, AX, ALU.add))
                step(V.tensor_scalar(nmean[:, par, :], mean[:, par, :], -1.0 / D, None, ALU.mult))
                V.tensor_tensor(xc[:, par, :, :], src, over_d(nmean[:, par, :]), ALU.add).then_inc(xc_ready, 1)

            def norm_var(n):
                dve.wait_ge(sq_ready, n + 1)
                V.tensor_reduce(var[:, n % 2, :], sq[:, :, :], AX, ALU.add).then_inc(var_ready, 1)

            def norm_scale(n):
                dve.wait_ge(rstd_ready, n + 1)
                dve.wait_ge(xc_ready, n + 1)
                if n >= B:
                    V.tensor_tensor(hn[:, n % 2, :, :].rearrange("p (c j) d -> p j c d", j=2),
                                    xc[:, n % 2, :, :].rearrange("p (j c) d -> p j c d", j=2),
                                    rstd[:, n % 2, :].rearrange("p (j c o) -> p j c o", j=2, o=1
                                                                ).to_broadcast([P, 2, NT // 2, D]),
                                    ALU.mult).then_inc(hn_ready, 1)
                    return
                V.tensor_tensor(hn[:, n % 2, :, :], xc[:, n % 2, :, :], over_d(rstd[:, n % 2, :]),
                                ALU.mult).then_inc(hn_ready, 1)

            def row_max(g, s, par):
                dve.wait_ge(s1_ready, g * NT + (s + 1))
                bank = S1A + 2 * (s % 2)
                V.tensor_reduce(nmax[:, par, s:s + 1], ps[:, bank:bank + 2, :].rearrange("p a n -> p (a n)"),
                                AX, ALU.max, negate=True).then_inc(s1_reduced[s % 2], 1)

            first = 0
            for b in range(B + 1):
                n = b - 1
                for u in range(2 * NT):
                    if b < B:
                        s, j, at = u // 2, u % 2, b * 2 * NT + u
                        if b == 0:
                            dve.wait_ge(gamma_loaded[s // 2], 16)
                        dve.wait_ge(tok_scored, at + 1)
                        if at >= 4:
                            dve.wait_ge(tok_summed, at - 3)
                        V.tensor_tensor(gated[:, at % 4, :], ps[:, at % 3, :],
                                        gamma_sb[:, s, HALF * j:HALF * (j + 1)], ALU.mult).then_inc(tok_gated, 1)
                    if u == 12 and b == 0:
                        small_tables()
                    for k in range(FIRST_MAXIMA.get(u, 0) if b == B else 0):
                        row_max(first // NT, first % NT, first // NT)
                        first += 1
                    if b == 0:
                        continue
                    h_n = h_all[:, NT * n:NT * (n + 1), :]
                    if u == 3:
                        dve.wait_ge(y_turned, b)
                        if n == 0:
                            dve.wait_ge(wide_loaded, 16)
                        bo_m = bo_b.rearrange("p (a b d) -> p a b d", a=1, b=1).to_broadcast([P, NT // 2, 2, D])
                        V.tensor_tensor(y_s[:, :, :].rearrange("p (j c) d -> p c j d", j=2),
                                        ps[:, 7, :].rearrange("p (c j d) -> p c j d", j=2, d=D), bo_m,
                                        ALU.add).then_inc(y_read, 1)
                        dve.wait_ge(y_read, b)
                        V.tensor_scalar(neg_s[:, :, :], y_s[:, :, :], 0.0, alpha, ALU.min, ALU.mult).then_inc(y_seq, 1)
                    if u == 4:
                        dve.wait_ge(y_seq, b)
                        V.scalar_tensor_tensor(out=h_n, in0=y_s[:, :, :], scalar=0.0, in1=neg_s[:, :, :],
                                               op0=ALU.max, op1=ALU.add).then_inc(h_ready, 1)
                        dve.wait_ge(h_ready, b)
                        norm_center(h_n, n)
                    if u == 7:
                        norm_var(n)
                    if u == 9:
                        norm_scale(n)
                    if u == 13:
                        dve.wait_ge(qk_h_ready, b)
                        dve.wait_ge(qk_m_ready, n)
                        V.scalar_tensor_tensor(out=qk_rest[:, :], in0=ps[:, 6:8, :].rearrange("p a n -> p (a n)"),
                                               scalar=qk_scale[:, 0:1], in1=qk_h[:, :], op0=ALU.mult,
                                               op1=ALU.subtract).then_inc(qk_r_ready, 1)
                    if u == 14:
                        dve.wait_ge(qk_r_ready, b)
                        dve.wait_ge(qk_m_ready, b)
                        dve.wait_ge(qk_stored[2], n * 2 * 16)
                        V.tensor_tensor(qk_l[:, :], qk_rest[:, :], qk_m[:, :], ALU.subtract).then_inc(qk_l_ready, 1)

            def normalize(n):
                dve.wait_ge(o_turned, n + 1)
                o_v = ps[:, MISC, 0:2 * P].rearrange("p (c j x) -> p c j x", c=2, x=VC)
                rec_v = o_rec[:, :].rearrange("p (c j o) -> p c j o", c=2, o=1)
                V.reciprocal(rec_v, o_v[:, :, :, DH:DH + 1]).then_inc(rec_ready, 1)
                dve.wait_ge(rec_ready, n + 1)
                V.tensor_tensor(attn[:, :, ds(n * DH, DH)].rearrange("p (j c) d -> p c j d", c=2),
                                o_v[:, :, :, 0:DH], rec_v.to_broadcast([P, 2, NT // 2, DH]),
                                ALU.mult).then_inc(o_normed, 1)

            def attention_copy(b):
                dve.wait_ge(ao_turned, b + 1)
                V.tensor_copy(ao_t[:, :], ps[:, 0, :]).then_inc(ao_t_copied, 1)

            def projection_copy(b):
                dve.wait_ge(proj_done, b + 1)
                V.tensor_scalar(pt_s[:, :], ps[:, 2, :], proj_b, None, ALU.add).then_inc(pt_copied, 1)

            def add_residual(b):
                h_b = h_all[:, NT * b:NT * (b + 1), :]
                dve.wait_ge(pt_turned, b + 1)
                V.tensor_tensor(h_b.rearrange("p (j c) d -> p c j d", j=2), h_b.rearrange("p (j c) d -> p c j d", j=2),
                                ps[:, 3, :].rearrange("p (c j d) -> p c j d", j=2, d=D),
                                ALU.add).then_inc(res_seq, 1)

            def center(b):
                dve.wait_ge(res_seq, b + 1)
                norm_center(h_all[:, NT * b:NT * (b + 1), :], B + b)

            def square_var(b):
                par = (B + b) % 2
                dve.wait_ge(xc_ready, B + b + 1)
                V.tensor_tensor(sq[:, :, :], xc[:, par, :, :], xc[:, par, :, :], ALU.mult).then_inc(sq_ready, 1)
                norm_var(B + b)

            def scale(b):
                norm_scale(B + b)

            def xn_affine(b):
                dve.wait_ge(xn_turned, b + 1)
                V.tensor_scalar(xf[:, b % 2, :], ps[:, 1, :], gam_c, bet_c, ALU.mult, ALU.add).then_inc(xf_ready, 1)
                dve.wait_ge(xf_ready, b + 1)
                V.tensor_copy(x_parts[:, b % 2, 0, :], xf[:, b % 2, :]).then_inc(x_rounded, 1)
                lower_parts(b)

            def lower_parts(b):
                par, part = b % 2, chain(part_seq, 2 * (b if b < 2 else 2))
                if b < 2:
                    dve.wait_ge(x_rounded, b + 1)
                else:
                    dve.wait_ge(xf_ready, b + 1)
                part(V.tensor_tensor(dve_rest, xf[:, par, :], x_parts[:, par, 0, :], ALU.subtract))
                part(V.tensor_copy(x_parts[:, par, 1, :], dve_rest))
                V.tensor_tensor(x_parts[:, par, 2, :], dve_rest, x_parts[:, par, 1, :],
                                ALU.subtract).then_inc(x_split[b], 1)

            WITHIN = {(2, 0): [(attention_copy, 0)], (2, 1): [(projection_copy, 0)], (2, 3): [(add_residual, 0), (center, 0)],
                      (2, 4): [(attention_copy, 1), (square_var, 0)], (2, 6): [(projection_copy, 1)],
                      (3, 0): [(add_residual, 1), (center, 1)], (3, 1): [(scale, 0), (square_var, 1)],
                      (3, 3): [(attention_copy, 2), (xn_affine, 0)], (3, 4): [(scale, 1)],
                      (3, 5): [(xn_affine, 1)], (3, 6): [(projection_copy, 2)]}

            def attend_dve(it, first, last):
                for u in range(RING):
                    g = it * RING + u
                    for s in range(NT):
                        if not (last and u >= RING - 2):
                            if s == 0:
                                dve.wait_ge(max_split, g + 1)
                            row_max(g + 2, s, u % 2)
                        if s == 5 and not (first and u == 0):
                            normalize(g - 1)
                        for stage, b in WITHIN.get((u, s), []) if last else []:
                            stage(b)

            attend_dve(0, True, False)
            with dve.Fori(1, G // RING - 1) as it:
                attend_dve(it, False, False)
            attend_dve(G // RING - 1, False, True)
            normalize(G - 1)
            add_residual(2)
            center(2)
            square_var(2)

            step = chain(route_seq, 0)

            def tiles(m, h):
                return m[:, RT * h:RT * (h + 1)]

            def tiles_e(m, h):
                return m[:, RT * h:RT * (h + 1), :]

            def over_e(m, h):
                return tiles(m, h).rearrange("p (m o) -> p m o", o=1).to_broadcast([P, RT, E])

            def first_of(logits, top, hot, h):
                step(V.tensor_reduce(tiles(top, h), tiles_e(logits, h), AX, ALU.max))
                step(V.tensor_tensor(tiles_e(eq, h), tiles_e(logits, h), over_e(top, h), ALU.is_equal))
                step(V.tensor_tensor(tiles_e(eq, h), tiles_e(eq, h), tiles_e(rank, h), ALU.mult))
                step(V.tensor_reduce(tiles(rk, h), tiles_e(eq, h), AX, ALU.max))
                step(V.tensor_tensor(tiles_e(hot, h), tiles_e(rank, h), over_e(rk, h), ALU.is_equal))

            def route_first(h):
                dve.wait_ge(lg_turned, h + 1)
                lg_v = ps[:, 7 if h else 5, :].rearrange("p (c t x) -> p c t x", t=4, x=VC)[:, :, :, 0:E]
                br_v = br_b.rearrange("p (c t e) -> p c t e", c=1, t=1).to_broadcast([P, NT // 2, 4, E])
                V.tensor_tensor(tiles_e(lg, h).rearrange("p (t c) e -> p c t e", t=4), lg_v, br_v,
                                ALU.add).then_inc(lg_read, 1)
                dve.wait_ge(lg_read, h + 1)
                first_of(lg, top1, hot1, h)

            def route_second(h):
                step(V.scalar_tensor_tensor(out=tiles_e(lg2, h), in0=tiles_e(hot1, h), scalar=LOWEST,
                                            in1=tiles_e(lg, h), op0=ALU.mult, op1=ALU.add))
                first_of(lg2, top2, hot2, h)
                V.tensor_tensor(tiles(gap, h), tiles(top2, h), tiles(top1, h), ALU.subtract).then_inc(gap_ready, 1)

            def route_weights(h):
                dve.wait_ge(e_gap_ready, h + 1)
                step(V.tensor_scalar(tiles(den, h), tiles(e_gap, h), 1.0, None, ALU.add))
                step(V.reciprocal(tiles(w_top1, h), tiles(den, h)))
                step(V.tensor_tensor(tiles(w_top2, h), tiles(w_top1, h), tiles(e_gap, h), ALU.mult))
                step(V.tensor_tensor(tiles_e(hot1, h), tiles_e(hot1, h), over_e(w_top1, h), ALU.mult))
                step(V.tensor_tensor(tiles_e(hot2, h), tiles_e(hot2, h), over_e(w_top2, h), ALU.mult))
                step(V.tensor_tensor(tiles_e(w_full, h), tiles_e(hot1, h), tiles_e(hot2, h), ALU.add))

            def route_parts(h):
                p0, p1, p2 = (w_p[:, h, :, :, E * i:E * (i + 1)].rearrange("p m k e -> p k m e") for i in range(PARTS))
                full, rest = (tiles_e(m, h).rearrange("p (k m) e -> p k m e", k=2) for m in (w_full, w_rest))
                step(V.tensor_copy(p0, full))
                step(V.tensor_tensor(rest, full, p0, ALU.subtract))
                step(V.tensor_copy(p1, rest))
                V.tensor_tensor(p2, rest, p1, ALU.subtract).then_inc(w_split, 1)

            route_first(0)
            add_residual(B - 1)
            norm_scale(2 * B - 2)
            route_second(0)
            route_weights(0)
            route_parts(0)
            center(B - 1)
            square_var(B - 1)

            def residual(n, i, stored):
                dve.wait_ge(ffn_done, n + 1)
                if stored is not None:
                    dve.wait_ge(out_stored[i], stored)
                ye_v = ps[:, 7, :].rearrange("p (m k d) -> p k m d", k=2, d=D)
                V.tensor_tensor(out_half, ye_v[:, 0], h_all[:, ds(n * (CH // P), CH // P), :],
                                ALU.add).then_inc(half_added, 1)
                dve.wait_ge(half_added, n + 1)
                V.tensor_tensor(out_s[:, i, :, :], ye_v[:, 1], out_half, ALU.add).then_inc(out_ready, 1)

            WITHIN = {(0, 2): [(scale, B - 1)], (1, 1): [(lower_parts, B - 1)], (2, 1): [(route_first, 1)], (2, 3): [(route_second, 1)],
                      (2, 5): [(route_weights, 1)], (2, 6): [(route_parts, 1)]}

            def experts_dve(c2, first, peeled):
                for i in range(2):
                    n = c2 * 2 + i
                    for e in range(E):
                        dve.wait_ge(hid_ready[(e // 2) % 2], n * 2 + (e // 4 + 1))
                        dve.wait_ge(spread_done, n * E + (e + 1))
                        if not (first and i == 0 and e < 4):
                            dve.wait_ge(down_done[e % 4], n * 2 + e // 4)
                        V.tensor_tensor(hid_w[:, e % 4, :], hid[:, (e // 2) % 2, CH * (e % 2):CH * (e % 2 + 1)],
                                        ps[:, 4 + e % 2, :], ALU.mult).then_inc(hid_scaled[e % 4], 1)
                        for stage, arg in WITHIN.get((n, e), []) if peeled else []:
                            stage(arg)
                        if e == 3 and not (first and i == 0):
                            residual(n - 1, 1 - i, None if first else c2 * 16 + (1 if i else -15))

            experts_dve(0, True, True)
            experts_dve(1, False, True)
            with dve.Fori(2, NCH // 2) as c2:
                experts_dve(c2, False, False)
            residual(NCH - 1, 1, 16 * (NCH // 2 - 1) + 1)

        @block.tensor
        def _(pe):
            mm = nc.tensor.matmul

            def turn_four(dst_bank, src, done):
                for c in range(NT // 2):
                    last = nc.tensor.transpose(ps[:, dst_bank, P * c:P * (c + 1)], src[:, P * c:P * (c + 1)],
                                               ident[:, :])
                last.then_inc(done, 1)

            def turn(src, bank, done):
                for m in range(NT):
                    c = m % (NT // 2)
                    last = nc.tensor.transpose(ps[0:D, bank + m // (NT // 2), P * c:P * (c + 1)], src(m), ident[:, :])
                last.then_inc(done, 1)

            def warm(times):
                zero = sq[:, :, :].rearrange("p m d -> p (m d)")
                for _ in range(times):
                    mm(ps[:, 7, 0:P], zero[:, 0:P], zero[:, 0:P], start=True, stop=True)

            pe.wait_ge(warm_ready, 1)
            warm(WARM[0])
            pe.wait_ge(tok_w_loaded, 16)
            mm(ps[0:D + 1, 3, 0:D + 1], wq_t, wk_t, start=True, stop=True)
            mm(ps[0:D + 1, 3, P:P + D], wv_t, wo_s, start=True, stop=True).then_inc(folded, 1)

            def project(b):
                pe.wait_ge(x_loaded[b], 16)
                pe.wait_ge(x_ones, b + 1)
                if b >= 2:
                    pe.wait_ge(v_pad_ready, b - 2)
                    pe.wait_ge(qk_r_ready, b - 2)
                for j in range(2):
                    last = mm(ps[0:KX, 4 + j, :], wqk[:, :], x_all[:, T * b + HALF * j:T * b + HALF * (j + 1)],
                              start=True, stop=True)
                last.then_inc(g_projected, 1)
                for j in range(2):
                    last = mm(ps[D * j:D * (j + 1), 6, :], wvo[:, :], x_all[:, T * b + HALF * j:T * b + HALF * (j + 1)],
                              start=True, stop=True)
                last.then_inc(vt_projected, 1)

            def turn_v(b):
                pe.wait_ge(vt_copied, b + 1)
                if b >= 2:
                    pe.wait_ge(y_read, b - 1)
                turn_four(7, vt_s, v_turned)

            warm(WARM[1])
            pe.wait_ge(folded_copied, 2)
            project(0)
            warm(WARM[2])
            pe.wait_ge(ident_ready, 1)
            turn_v(0)

            def score(at):
                b, u = at // (2 * NT), at % (2 * NT)
                s, j = u // 2, u % 2
                if u == 0:
                    pe.wait_ge(g_copied, b + 1)
                if at >= 3:
                    pe.wait_ge(tok_gated, at - 2)
                mm(ps[:, at % 3, :], x_all[:, T * b + P * s:T * b + P * (s + 1)],
                   g_t[:, b % 2, HALF * j:HALF * (j + 1)], start=True, stop=True).then_inc(tok_scored, 1)

            def retain(at):
                b, u = at // (2 * NT), at % (2 * NT)
                s, j = u // 2, u % 2
                if u == 0:
                    pe.wait_ge(v_copied, b + 1)
                    pe.wait_ge(ret_copied, b)
                pe.wait_ge(tok_gated, at + 1)
                mm(ps[D * j:D * (j + 1), 3, :], v_s[:, b % 2, s, :], gated[:, at % 4, :], start=(s == 0),
                   stop=(s == NT - 1)).then_inc(tok_summed, 1)

            def scores_by_query(g, s, u):
                pe.wait_ge(s1_reduced[s % 2], g * (NT // 2) + s // 2)
                bank = S1A + 2 * (s % 2)
                for j in range(2):
                    last = mm(ps[:, bank + j, :], q_ring[0:MAXROW, u, P * s:P * (s + 1)],
                              k_ring[0:MAXROW, u, HALF * j:HALF * (j + 1)], start=True, stop=(s > 0 or j == 0))
                if s == 0:
                    for i in range(PARTS):
                        last = mm(ps[:, bank + 1, HALF - P:HALF], flip_b[:, :], x_ring[:, u, i, :],
                                  start=False, stop=(i == PARTS - 1))
                last.then_inc(s1_ready, 1)

            def turn_maxima(g, par):
                pe.wait_ge(max_split, g + 1)
                nc.tensor.transpose(max_ps, max_p[:, par, :, :].rearrange("p a m -> p (a m)"),
                                    ident_b[:, :]).then_inc(max_turned[par], 1)

            for at in range(2):
                score(at)
            first = 0
            for b in range(B + 1):
                n = b - 1
                for u in range(2 * NT):
                    at = b * 2 * NT + u
                    if u % 2 == 0:
                        for k in range(2):
                            if at + 2 + k < B * 2 * NT:
                                score(at + 2 + k)
                        for k in range(2):
                            if b < B:
                                retain(at + k)
                    if u == 2 and b > 0:
                        pe.wait_ge(ret_copied, b)
                        pe.wait_ge(qk_r_ready, n)
                        turn_four(7, ret_t, y_turned)
                    if u == 4 and b + 1 < B:
                        project(b + 1)
                    if u == 8 and b + 1 < B:
                        turn_v(b + 1)
                    if u == 10 and b > 0:
                        pe.wait_ge(hn_ready, b)
                        if b + 1 < B:
                            pe.wait_ge(g_copied, b + 2)
                        pe.wait_ge(v_pad_ready, n)
                        turn(lambda m: hn[:, n % 2, m, :], 4, hn_turned)
                    if u == 12 and b > 0:
                        if n == 0:
                            pe.wait_ge(aug_loaded, 16)
                        pe.wait_ge(hn_t_copied, b)
                        pe.wait_ge(y_read, b)
                        if b + 1 < B:
                            pe.wait_ge(vt_copied, b + 2)
                            pe.wait_ge(v_copied, b + 2)
                        for j in range(2):
                            last = mm(ps[:, 6 + j, :], qk_w, hn_t[:, HALF * j:HALF * (j + 1)], start=True, stop=True)
                        last.then_inc(qk_done, 1)
                        for j in range(2):
                            last = mm(ps[D * j:D * (j + 1), 4, :], vv_w, hn_t[:, HALF * j:HALF * (j + 1)],
                                      start=True, stop=True)
                        last.then_inc(vv_done, 1)
                    if u == 14 and b > 0:
                        pe.wait_ge(vv_copied, b)
                        turn_four(5, vv_t, vv_turned)
                    for k in range(FIRST_SCORES.get(u, 0) if b == B else 0):
                        if first == 0:
                            pe.wait_ge(consts_ready, 1)
                            pe.wait_ge(tok_gated, B * 2 * NT)
                        if first == 1:
                            pe.wait_ge(ret_copied, B)
                        if first % NT == 0:
                            pe.wait_ge(operands[first // NT], 16 * N_OPERANDS)
                        scores_by_query(first // NT, first % NT, first // NT)
                        first += 1
                    if u == 14 and b == B:
                        pe.wait_ge(qk_r_ready, B)
                        turn_maxima(0, 0)
            pe.wait_ge(qk_r_ready, B)
            pe.wait_ge(v_pad_ready, B)

            def scores_by_key(g, s, u):
                for j in range(2):
                    pe.wait_ge(exp_done[j], g * NT + (s + 1))
                    corner = s == NT - 1 and j == 0
                    last = mm(ps[:, S2A + j, :], k_ring[0:MAXROW + PARTS, u, P * s:P * (s + 1)],
                              q_ring[0:MAXROW + PARTS, u, HALF * j:HALF * (j + 1)], start=True, stop=not corner)
                    if corner:
                        for i in range(PARTS):
                            last = mm(ps[:, S2A, 0:P], x_ring[:, u, i, :], flip_b[:, :], start=False,
                                      stop=(i == PARTS - 1))
                    last.then_inc(s2_ready, 1)

            def values(it, g, m, u):
                if m == 0 and not (isinstance(g, int) and g == 0):
                    pe.wait_ge(o_copied[(u - 1) % RING], it + (2 if u else 1))
                for j in range(2):
                    pe.wait_ge(exp_done[j], g * NT + (m + 2))
                for j in range(4):
                    last = mm(ps[VC * j:VC * (j + 1), PVB, 0:2 * P], v_ring[:, u, m, :],
                              probs[:, m % 4, 2 * P * j:2 * P * (j + 1)], start=(m == 0), stop=(m == NT - 1))
                last.then_inc(pv_done[m % 4], 1)

            def turn_output(before, copied, maxima):
                pe.wait_ge(o_copied[before], copied)
                pe.wait_ge(max_copied, maxima)
                for c in range(2):
                    last = nc.tensor.transpose(ps[:, MISC, P * c:P * (c + 1)], o_t[:, P * c:P * (c + 1)], ident[:, :])
                last.then_inc(o_turned, 1)

            def turn_attention(b):
                if b == 0:
                    for i in range(2):
                        pe.wait_ge(s1_reduced[i], G * NT // 2)
                    pe.wait_ge(weights_padded, 1)
                for c in range(NT // 2):
                    for j in range(2):
                        last = mm(ps[D * j:D * (j + 1), 0, P * c:P * (c + 1)],
                                  attn[:, NT // 2 * j + c, D * b:D * (b + 1)], ident[:, :], start=True, stop=True)
                last.then_inc(ao_turned, 1)

            def project_attention(b):
                pe.wait_ge(ao_t_copied, b + 1)
                mm(ps[:, 2, :], proj2[:, :], ao_t[:, :], start=True, stop=True).then_inc(proj_done, 1)

            def turn_projection(b):
                pe.wait_ge(pt_copied, b + 1)
                pe.wait_ge(res_seq, b)
                turn_four(3, pt_s, pt_turned)

            def turn_norm(b):
                pe.wait_ge(hn_ready, B + b + 1)
                pe.wait_ge(xf_ready, b)
                for c in range(NT // 2):
                    last = nc.tensor.transpose(ps[:, 7 if b >= 2 else 1, P * c:P * (c + 1)],
                                               hn[:, b % 2, 2 * c:2 * c + 2, :].rearrange("p m d -> p (m d)"),
                                               ident[:, :])
                last.then_inc(xn_turned, 1)

            def logits(b):
                pe.wait_ge(x_placed[b], 8 * 16)
                pe.wait_ge(up_split, 1)
                if b >= 2:
                    pe.wait_ge(xf_ready, B)
                for k in range(PARTS):
                    for j in range(2):
                        t = 2 * (b % 2) + j
                        last = mm(ps[VC * t:VC * (t + 1), 7 if b >= 2 else 4, :], up_p[:, k, UPS:],
                                  (x2_all if k == 2 else x1_all)[:, T * b + HALF * j:T * b + HALF * (j + 1)],
                                  start=(k == 0), stop=(k == PARTS - 1))
                last.then_inc(routed, 1)

            def turn_logits(h):
                pe.wait_ge(lg_t_copied, h + 1)
                turn_four(7 if h else 5, lg_t, lg_turned)

            def turn_weights(h):
                pe.wait_ge(w_split, h + 1)
                for m in range(NT):
                    last = nc.tensor.transpose(
                        ps[:, 7 if h else 6, :].bitcast(bf16)[0:2 * VC, P * m:P * (m + 1)],
                        w_p[:, h, m, :, :].rearrange("p k x -> p (k x)"), ident_b[:, :])
                last.then_inc(w_turned, 1)

            WITHIN = {(2, 0): [(turn_attention, 0)], (2, 1): [(project_attention, 0)], (2, 3): [(turn_projection, 0)],
                      (2, 4): [(turn_attention, 1)], (2, 6): [(project_attention, 1)],
                      (3, 0): [(turn_projection, 1)], (3, 2): [(turn_norm, 0)], (3, 3): [(turn_attention, 2)],
                      (3, 5): [(turn_norm, 1)], (3, 6): [(project_attention, 2)], (3, 7): [(turn_projection, 2)]}

            def attend_pe(it, first, last):
                for u in range(RING):
                    g = it * RING + u
                    ahead = not (last and u >= RING - 2)
                    start, end = first and u == 0, last and u == RING - 1
                    pe.wait_ge(max_rows[u], it * 16 + 16)
                    pe.wait_ge(values_loaded[u], it * 16 + 16)
                    if ahead:
                        pe.wait_ge(operands[(u + 2) % RING],
                                   (it + (u + 2) // RING) * (16 * N_OPERANDS) + 16 * N_OPERANDS)
                    for s in range(NT):
                        scores_by_key(g, s, u)
                        if s == 1 and not start:
                            values(it, g - 1, NT - 1, (u - 1) % RING)
                        if ahead:
                            scores_by_query(g + 2, s, (u + 2) % RING)
                        if s == 0 and not start:
                            values(it, g - 1, NT - 2, (u - 1) % RING)
                        if s > 1:
                            values(it, g, s - 2, u)
                        if s == 1 and not end:
                            if not (first and u < 2):
                                pe.wait_ge(o_normed, g - 1)
                            turn_maxima(g + 1, (u + 1) % 2)
                        if s == 4 and end:
                            pe.wait_ge(o_normed, g - 1)
                        if s == 4 and not start:
                            turn_output((u - 1) % RING, it + (2 if u else 1), G if end else g + 2)
                        for stage, b in WITHIN.get((u, s), []) if last else []:
                            stage(b)

            attend_pe(0, True, False)
            with pe.Fori(1, G // RING - 1) as it:
                attend_pe(it, False, False)
            attend_pe(G // RING - 1, False, True)
            for m in (NT - 2, NT - 1):
                values(G // RING - 1, G - 1, m, RING - 1)
            pe.wait_ge(o_normed, G - 1)
            turn_output(RING - 1, G // RING + 1, G)

            pe.wait_ge(b2_ready, 1)
            for j in range(2):
                pe.wait_ge(exp_done[j], G * NT + 1)
            pe.wait_ge(o_normed, G)
            turn_attention(B - 1)
            project_attention(B - 1)
            for b in range(2):
                logits(b)
            turn_projection(B - 1)
            turn_logits(0)

            def down(n, e):
                pe.wait_ge(hid_scaled[e % 4], n * 2 + (e // 4 + 1))
                mm(ps[D * (e % 2):D * (e % 2 + 1), 6, :], w2_s[:, e, :], hid_w[:, e % 4, :],
                   start=(e < 2), stop=(e >= E - 2)).then_inc(down_done[e % 4], 1)

            def down_bias(n):
                for k in range(PARTS):
                    mm(ps[0:D, 6, :], b2_p[:, k, :], wt_all[:, ds(n * CH, CH)],
                       start=False, stop=False)

            def finish(n, first):
                if not first:
                    pe.wait_ge(out_ready, n)
                pe.wait_ge(ye_copied, n + 1)
                turn_four(7, ye_t, ffn_done)

            def up(n, e2):
                for k in range(2):
                    for i in range(PARTS):
                        last = mm(ps[:, 2 * (e2 % 2) + k, :], up_p[:, i, HID * (2 * e2 + k):HID * (2 * e2 + k + 1)],
                                  (x2_all if i == 2 else x1_all)[:, ds(n * CH, CH)], start=(i == 0),
                                  stop=(i == PARTS - 1))
                last.then_inc(up_done, 1)

            def experts_pe(c2, first, peeled):
                for i in range(2):
                    n = c2 * 2 + i
                    start = first and i == 0
                    for e2 in range(E // 2):
                        if not (start and e2 < 2):
                            pe.wait_ge(hid_ready[e2 % 2], n * 2 + e2 // 2)
                            up(n, e2)
                        if start and e2 == 0:
                            up(n, 0)
                            pe.wait_ge(res_seq, B)
                            up(n, 1)
                            turn_weights(0)
                            turn_norm(B - 2)
                            pe.wait_ge(w_t_copied, 1)
                        for e in (2 * e2, 2 * e2 + 1):
                            if not (start and e < 2):
                                pe.wait_ge(hid_scaled[(e - 2) % 4], n * 2 + (e + 2) // 4)
                            mm(ps[:, 4 + e % 2, :], pick[:, e, :], wt_all[:, ds(n * CH, CH)], start=True,
                               stop=True).then_inc(spread_done, 1)
                        for k in range(2):
                            if e2:
                                if e2 == 1 and k == 0 and start:
                                    pe.wait_ge(w_t_copied, 2)
                                if e2 == 1 and k == 0 and not start:
                                    pe.wait_ge(ye_copied, n)
                                down(n, 2 * e2 - 2 + k)
                            elif not start:
                                down(n - 1, E - 2 + k)
                        if e2 == 2:
                            down_bias(n)
                        if peeled and n == 0 and e2 == 2:
                            turn_norm(B - 1)
                        if peeled and n == 1 and e2 == 3:
                            pe.wait_ge(out_ready, 1)
                            for b in range(2, B):
                                logits(b)
                        if peeled and n == 2 and e2 == 0:
                            turn_logits(1)
                        if peeled and n == 3 and e2 == 0:
                            pe.wait_ge(out_ready, 2)
                            turn_weights(1)
                        if e2 == 1 and not start:
                            if peeled and n == 1:
                                pe.wait_ge(xf_ready, B)
                            elif peeled and n == 2:
                                pe.wait_ge(lg_read, 2)
                            else:
                                pe.wait_ge(w_t_copied, B)
                            finish(n - 1, first and i == 1)

            experts_pe(0, True, True)
            experts_pe(1, False, True)
            with pe.Fori(2, NCH // 2) as c2:
                experts_pe(c2, False, False)
            for k in range(2):
                down(NCH - 1, E - 2 + k)
            finish(NCH - 1, False)


def kernel(**inputs):
    import concourse.bacc as bacc
    from concourse.bass_utils import run_bass_kernel_spmd

    a = {k: np.asarray(v) for k, v in inputs.items()}
    x = a["x"]
    tok = lambda n: a["L0_tok_" + n]
    att = lambda n: a["L0_attn_" + n]
    ffn = lambda n: a["L0_ffn_" + n]
    def aug(w, bias):
        return np.concatenate([w, bias.reshape(1, -1)], axis=0)

    def twice(w):
        return np.concatenate([w.reshape(w.shape[0], -1)] * 2, axis=0)

    w1 = ffn("W1")
    w2 = ffn("W2")
    arrays = {
        "x_t": x.reshape(-1, x.shape[-1]).T,
        "gamma_t": tok("d_gamma_batched").T,
        "tok_pack": np.concatenate([aug(tok("Wq"), tok("bq")).T, aug(tok("Wk"), tok("bk")).T,
                                    aug(tok("Wv"), tok("bv")).T, tok("Wo")], axis=1),
        "aug_pack": aug(att("qkv_w"), att("qkv_b")),
        "up_pack": twice(np.concatenate([w1.transpose(1, 0, 2).reshape(w1.shape[1], -1), ffn("Wr")], axis=1)),
        "wide_pack": np.concatenate([w2.transpose(1, 0, 2).reshape(w2.shape[1], -1),
                                     np.broadcast_to(tok("bo"), (w2.shape[1], tok("bo").size)),
                                     np.broadcast_to(tok("prelu_a").reshape(1, 1), (w2.shape[1], 1)),
                                     twice(att("proj_w")), twice(att("proj_b")), twice(ffn("gamma")),
                                     twice(ffn("beta")),
                                     np.broadcast_to(ffn("br"), (w2.shape[1], ffn("br").size)),
                                     ffn("b1").reshape(w1.shape[0], -1).T], axis=1),
        "b2_rows": np.concatenate([ffn("b2")] * 3, axis=0),
        "rpb_rev": att("rpb_table").T[:, ::-1],
    }
    nc = bacc.Bacc("TRN2", target_bir_lowering=False, num_devices=1)
    feeds, args = {}, []
    for name, v in arrays.items():
        v = np.ascontiguousarray(v)
        feeds[name] = v
        args.append(nc.dram_tensor(name, v.shape, mybir.dt.from_np(v.dtype), kind="ExternalInput").ap())
    out = nc.dram_tensor("out", (x.size // x.shape[-1], x.shape[-1]), mybir.dt.float32, kind="ExternalOutput").ap()
    vit_tower_kernel(nc, *args, out)
    r = run_bass_kernel_spmd(nc, [feeds], core_ids=[0])
    return r.results[0]["out"].reshape(x.shape[0], x.shape[2], x.shape[3])
```
